# Optimizing a Trainium2 kernel written in Bass

```python
import numpy as np
import jax
import jax.numpy as jnp

def _softmax(x, axis=-1):
    return jax.nn.softmax(x, axis=axis)

def _gelu(x):
    return jax.nn.gelu(x, approximate=True)

def _silu(x):
    return jax.nn.silu(x)

def _sigmoid(x):
    return jax.nn.sigmoid(x)

def _layernorm(x, axis=-1, eps=1e-05):
    m = jnp.mean(x, axis=axis, keepdims=True)
    v = jnp.var(x, axis=axis, keepdims=True)
    return (x - m) / jnp.sqrt(v + eps)

def _scatter_add(tgt, idx, src, axis=0):
    return tgt.at[idx].add(src)

def _segment_sum(src, seg, n):
    return jax.ops.segment_sum(src, seg, n)
kernel_name = 'mk_gnn_preln_d1_gnn_r8_b2c915'

def setup_inputs(seed: int=0):
    np.random.seed(seed)
    _w = jnp.asarray

    def _rec_inputs():
        import jax
        import jax.numpy as jnp
        _gk = jax.random.key(seed)
        x = -0.000202 + 1 * jax.random.normal(jax.random.fold_in(_gk, 1), (6250, 128), jnp.float32)
        src = jax.random.randint(jax.random.fold_in(_gk, 2), (100000,), 0, 6250, jnp.int32)
        dst = jax.random.randint(jax.random.fold_in(_gk, 3), (100000,), 0, 6250, jnp.int32)
        _o = jnp.argsort(dst, stable=True)
        src = src[_o]
        dst = dst[_o]
        edge_attr_128 = 9.41057e-06 + 1 * jax.random.normal(jax.random.fold_in(_gk, 11), (100000, 128), jnp.float32)
        return (x, src, dst, edge_attr_128)
    x, src, dst, edge_attr_128 = _rec_inputs()

    def _L0_gnn_setup():
        import jax, jax.numpy as jnp
        import numpy as np
        ALPHA = 0.2
        N_NODES = 6250
        N_EDGES = 200000
        IN_F = 128
        OUT_F = 128
        key = jax.random.key(seed)
        k1, k2, k3, k4, k5 = jax.random.split(key, 5)
        x = jax.random.normal(k1, (N_NODES, IN_F), dtype=jnp.float32)
        edge = jax.random.randint(k2, (2, N_EDGES), 0, N_NODES, dtype=jnp.int64)
        edge_embed = jax.random.normal(k3, (N_EDGES, OUT_F), dtype=jnp.float32)
        a = jax.random.normal(k4, (OUT_F, IN_F + OUT_F), dtype=jnp.float32) * (1.414 * np.sqrt(2.0 / (OUT_F + IN_F + OUT_F)))
        a_2 = jax.random.normal(k5, (1, OUT_F), dtype=jnp.float32) * (1.414 * np.sqrt(2.0 / (1 + OUT_F)))
        return {'x': x, 'edge': edge, 'edge_embed': edge_embed, 'a': a, 'a_2': a_2}
    _L0_gnn_all = _L0_gnn_setup()
    _L0_gnn_in = {k: v for k, v in _L0_gnn_all.items() if k in ('a', 'a_2')}
    del _L0_gnn_all
    return {'x': x, 'src': src, 'dst': dst, 'edge_attr_128': edge_attr_128, 'L0_gnn_a': _L0_gnn_in['a'], 'L0_gnn_a_2': _L0_gnn_in['a_2']}

def reference(x, src, dst, edge_attr_128, L0_gnn_a, L0_gnn_a_2):
    import jax
    import jax.numpy as jnp

    def _L0_gnn_ref(x, edge, edge_embed, a, a_2):
        import jax, jax.numpy as jnp
        import numpy as np
        ALPHA = 0.2
        N_NODES = 6250
        N_EDGES = 200000
        IN_F = 128
        OUT_F = 128
        n_nodes = x.shape[0]
        src = edge[0]
        edge_h = jnp.concatenate([x[src], edge_embed], axis=1)
        edge_m = jnp.einsum('ef,of->eo', edge_h, a)
        powers = -jax.nn.leaky_relu(edge_m @ a_2[0], negative_slope=ALPHA)
        edge_e = jnp.exp(powers)
        e_rowsum = jax.ops.segment_sum(edge_e, src, num_segments=n_nodes)
        e_rowsum = jnp.where(e_rowsum == 0.0, 1e-12, e_rowsum)
        h_prime = jax.ops.segment_sum(edge_e[:, None] * edge_m, src, num_segments=n_nodes)
        return h_prime / e_rowsum[:, None]
    edge_index = jnp.stack([src, dst])
    h = jnp.maximum(_layernorm(x, axis=-1), 0.0)
    x = x + _L0_gnn_ref(h, edge_index, edge_attr_128, L0_gnn_a, L0_gnn_a_2)
    return x

_drawn_inputs = setup_inputs


def setup_inputs(seed=0):
    import zlib

    import numpy as np

    out = dict(_drawn_inputs(seed))
    spreads = {}
    factors = {}
    for name, (base, spread) in spreads.items():
        noise = np.random.default_rng([zlib.crc32(name.encode()), seed]).standard_normal(out[name].shape)
        drawn = base * np.exp(spread * noise) if base else spread * noise
        out[name] = jnp.asarray(drawn.astype(out[name].dtype))
    for name, factor in factors.items():
        out[name] = (out[name] * factor).astype(out[name].dtype)
    return out
```

```python
from contextlib import ExitStack

import numpy as np

import concourse.bass as bass
from concourse import mybir

ALU = mybir.AluOpType
ACT = mybir.ActivationFunctionType
F32 = mybir.dt.float32
BF16 = mybir.dt.bfloat16
I16 = mybir.dt.int16
I32 = mybir.dt.int32
U32 = mybir.dt.uint32
AX_X = mybir.AxisListType.X
ENGINE = mybir.EngineType

P = 128
NODES, EDGES, FEAT = 6250, 100000, 128
EPS = 1e-5
SLOPE = 0.2
TINY = 1e-12

WINDOWS = -(-NODES // P)
BUCKETS = WINDOWS + 1
LAST_ROWS = NODES - (WINDOWS - 1) * P

COLS = EDGES // P
TAIL = EDGES - COLS * P
GT = 8
RG = 7
RT = GT * RG
ROUNDS = -(-(COLS + 1) // RT)
TILES = ROUNDS * RT
GROUPS = ROUNDS * RG
LAST_FULL = COLS - (GROUPS - 1) * GT

CHUNKS = [2, 4, 4, 2, 2]
assert sum(CHUNKS) == ROUNDS and RT >= BUCKETS - 1
FIRST = [sum(CHUNKS[:c]) for c in range(len(CHUNKS))]
STEP_ROUND = [FIRST[c] + c for c in range(len(CHUNKS))]
STEP_ROUNDS = ROUNDS + len(CHUNKS)
STEPS = STEP_ROUNDS * RG
MAXT = max(CHUNKS) * RT

SLOTS = 2 * RG
ROW = FEAT + 4
ONE, SRC, SCORE = FEAT, FEAT + 1, FEAT + 2
TSTEP = 2 * GT
WRING = 14
BB = 10
JUNK = 4
PER_BANK = 3
NO_CHECK = "the table's entries are clamped on chip"

PLAN = [
    ("rank", 0), ("feed", 0, 2), ("rank", 1), ("feed", 2, 2), ("rank", 2), ("feed", 4, 1),
    ("rank", 3), ("rank", 4), ("norm",), ("feed", 5, 1),
    ("pairs", 0), ("feed", 6, 1), ("feed", 7, 1), ("pairs", 1, 2), ("feed", 8, 1), ("pairs", 1, 3),
    ("feed", 9, 1), ("pairs", 1, 5), ("feed", 10, 1), ("feed", 11, 1), ("pairs", 2, 2),
    ("feed", 12, 1), ("pairs", 2, 4), ("feed", 13, 1), ("pairs", 2, 5), ("pairs", 3), ("pairs", 4),
]


def gnn_kernel(nc, x, src, edge_attr, a, a_2, out):
    ctx = ExitStack()
    with ctx:
        def sb(name, shape, dt):
            return ctx.enter_context(nc.sbuf_tensor(name, shape, dt))

        def sem(name):
            return ctx.enter_context(nc.semaphore(name))

        ordered = nc.dram_tensor("ordered_rows", [TILES * P, ROW], F32, kind="Internal").ap()
        self_part = nc.dram_tensor("self_part", [P, WINDOWS * ROW], F32, kind="Internal").ap()

        feed = sb("feed", [P, SLOTS * GT * ROW], F32)
        back = sb("back", [P, SLOTS * GT * ROW], F32)
        acc = sb("acc", [P, BUCKETS * ROW], F32)
        node_score = sb("node_score", [P, BUCKETS * ROW], F32)
        node_id = sb("node_id", [P, BUCKETS * ROW], I16)
        table = sb("table", [1, STEPS * TSTEP], I32)
        weighted = sb("weighted", [P, WRING, P], F32)
        dist = sb("dist", [P, GT, P], BF16)
        src_row = sb("src_row", [P, TILES], I32)
        src16 = sb("src16", [P, TILES], I16)
        bucket = sb("bucket", [P, TILES], BF16)
        dest = sb("dest", [P, SLOTS * GT], U32)
        junk = sb("junk", [P, JUNK, P], F32)
        junk2 = sb("junk2", [P, JUNK, P], F32)
        edge_w = sb("edge_w", [P, FEAT], F32)
        node_w = sb("node_w", [P, P], F32)
        A2T = sb("A2T", [P, FEAT], F32)
        A1T = sb("A1T", [P, FEAT], F32)
        ident = sb("ident", [P, P], F32)
        below = sb("below", [P, P], BF16)
        above = sb("above", [P, P], BF16)
        ones_bf = sb("ones_bf", [P, 1], BF16)
        bucket_no = sb("bucket_no", [P, BUCKETS], F32)
        bucket_col = sb("bucket_col", [BUCKETS, 1], F32)
        ends = sb("ends", [P, BUCKETS + 1], BF16)
        shift = sb("shift", [P, BUCKETS], F32)
        first_pair = sb("first_pair", [BUCKETS, 4], F32)
        first_pair_i = sb("first_pair_i", [BUCKETS, 1], I32)
        zsum = sb("zsum", [P, 2, GT], F32)
        zed = sb("zed", [P, 2, GT], F32)
        neg_leaky = sb("neg_leaky", [P, 2, GT], F32)
        prob = sb("prob", [P, 2, GT], F32)
        neg_prob = sb("neg_prob", [P, 2, GT], F32)
        moments = sb("moments", [P, WINDOWS, 2], F32)
        eps_col = sb("eps_col", [P, 1], F32)
        rstd = sb("rstd", [P, WINDOWS], F32)
        shift_n = sb("shift_n", [P, WINDOWS], F32)
        denom = sb("denom", [P, WINDOWS], F32)
        inv = sb("inv", [P, WINDOWS], F32)
        kept = sb("kept", [P, WINDOWS], F32)

        half = back[:, :].bitcast(BF16)
        hot = half[:, 0:BUCKETS * MAXT]
        count = half[:, BUCKETS * MAXT:2 * BUCKETS * MAXT]
        f0 = BUCKETS * MAXT
        picked = back[:, f0:f0 + BB * MAXT]
        partial = back[:, f0 + BB * MAXT:f0 + (BB + 5) * MAXT]
        rank = back[:, f0 + (BB + 5) * MAXT:f0 + (BB + 6) * MAXT]
        assert f0 + (BB + 6) * MAXT <= SLOTS * GT * ROW and BUCKETS == 5 * BB
        rank_i = picked[:, 0:MAXT].bitcast(I32)
        part_a = picked[:, MAXT:2 * MAXT].bitcast(I32)
        part_b = picked[:, 2 * MAXT:3 * MAXT].bitcast(I32)
        part_c = picked[:, 3 * MAXT:4 * MAXT].bitcast(I32)
        row1 = picked[0:1, 4 * MAXT:6 * MAXT]
        row2 = picked[0:1, 6 * MAXT:8 * MAXT]
        row3 = picked[0:1, 8 * MAXT:10 * MAXT]
        pair_no = sb("pair_no", [BUCKETS, MAXT + RT], F32)
        started = sb("started", [BUCKETS, MAXT + RT], BF16)
        a_sb = weighted[:, 0:2, :].rearrange("p c f -> p (c f)")
        a2_row = weighted[0:1, 2, :]
        ones_row = weighted[0:1, 3, :]
        a2_wide = weighted[:, 4, :]
        h_st = weighted[:, 6:8, :]
        hT_st = weighted[:, 8:10, :]
        stats = back[:, 0:6 * WINDOWS]

        psum = ctx.enter_context(nc.psum_tensor("psum", [P, 8 * 512], F32))

        def bank(b, lo, n, rows=P):
            return psum[0:rows, b * 512 + lo:b * 512 + lo + n]

        x_loaded = sem("x_loaded")
        a_loaded = sem("a_loaded")
        src_loaded = sem("src_loaded")
        pool_set = sem("pool_set")
        load_sem = [sem(f"load{k}") for k in range(RG)]
        landed = sem("landed")
        fed = sem("fed")
        released = sem("released")
        scattered = [sem(f"scattered{k}") for k in range(RG)]
        back_sem = [sem(f"back{k}") for k in range(RG)]
        vec = sem("vec")
        hots_done = sem("hots_done")
        ends_done = sem("ends_done")
        shift_done = sem("shift_done")
        base_taken = sem("base_taken")
        started_done = sem("started_done")
        pairs_done = sem("pairs_done")
        table_done = sem("table_done")
        weights_step = sem("weights_step")
        weights_copied = sem("weights_copied")
        stats_done = sem("stats_done")
        var_done = sem("var_done")
        std_done = sem("std_done")
        norm_done = sem("norm_done")
        h_done = sem("h_done")
        hT_done = sem("hT_done")
        hT_copied = sem("hT_copied")
        self_done = sem("self_done")
        self_copied = sem("self_copied")
        self_saved = sem("self_saved")
        acc_zero = sem("acc_zero")
        edge_dots = sem("edge_dots")
        node_sums = sem("node_sums")
        z_done = sem("z_done")
        leaky_done = sem("leaky_done")
        dist_done = sem("dist_done")
        prob_done = sem("prob_done")
        weighted_done = sem("weighted_done")
        product_done = sem("product_done")
        acc_done = sem("acc_done")
        inv_done = sem("inv_done")
        scaled_done = sem("scaled_done")
        scaledT_done = sem("scaledT_done")
        scaledT_copied = sem("scaledT_copied")
        out_ready = sem("out_ready")
        self_added = sem("self_added")
        result_done = sem("result_done")
        final_loaded = sem("final_loaded")
        stored = sem("stored")

        feed_g = feed[:, :].rearrange("p (g r) -> p g r", r=GT * ROW)
        back_g = back[:, :].rearrange("p (g r) -> p g r", r=GT * ROW)
        edge_cols = edge_attr[0:COLS * P, :].rearrange("(p t) f -> p t f", t=COLS)
        ordered_g = ordered.rearrange("(g p u) r -> g p (u r)", p=P, u=GT)
        acc_w = acc[:, :].rearrange("p (w r) -> p w r", r=ROW)

        fin_self = feed[:, 0:WINDOWS * ROW].rearrange("p (w r) -> p w r", r=ROW)
        fin_x = feed[:, WINDOWS * ROW:2 * WINDOWS * ROW].rearrange("p (w r) -> p w r", r=ROW)
        scaled = weighted[:, 0:RG, :]
        scaledT = weighted[:, RG:2 * RG, :]

        def x_windows(dst):
            whole = x[0:(WINDOWS - 1) * P, :].rearrange("(w p) f -> p w f", p=P)
            return ((dst[:, 0:WINDOWS - 1, 0:FEAT], whole),
                    (dst[0:LAST_ROWS, WINDOWS - 1, 0:FEAT], x[(WINDOWS - 1) * P:NODES, :]))

        def back_slot(c, r, k):
            return ((FIRST[c] + r) % 2) * RG + k

        def load_pairs(engine, step, what, n=GT):
            got = []
            for lo in range(0, n, 4):
                ap = table[0:1, bass.ds(step * TSTEP + what * GT + lo, 4)]
                _, vals = nc.values_load_multi_w_load_instructions(
                    ap, engines=[engine], min_val=0,
                    max_val=((BUCKETS - 1) if what == 0 else (SLOTS * GT - 1)) * ROW,
                    skip_runtime_bounds_check_because=NO_CHECK)
                got += vals
            return got

        block = ctx.enter_context(nc.Block())

        @block.sync
        def _(sp):
            def load(g, slot, k):
                dst = feed_g[:, bass.ds(slot, 1), :].rearrange("p g (u r) -> p (g u) r", r=ROW)[:, :, 0:FEAT]
                sp.dma_start(dst, edge_cols[:, bass.ds(g * GT, GT), :]).then_inc(load_sem[k], 16)

            sp.dma_start(src_row[:, 0:COLS], src[0:COLS * P].rearrange("(p t) -> p t", t=COLS)).then_inc(src_loaded, 16)
            for k in range(RG):
                load(k, k, k)
                if k == 0:
                    sp.wait_ge(pool_set, 1)
                    sp.dma_start(src_row[0:TAIL, COLS:COLS + 1],
                                 src[COLS * P:EDGES].rearrange("(p t) -> p t", t=1)).then_inc(src_loaded, 16)

            def pass_on(r, k, scatter_rounds):
                sp.wait_ge(load_sem[k], 16 * (r + 1))
                sp.sem_inc(landed, 1)
                if scatter_rounds:
                    sp.wait_ge(scattered[k], 16 * GT * r)

            for k in range(RG):
                pass_on(0, k, False)
                load(RG + k, RG + k, k)
            with sp.Fori(1, ROUNDS - 2) as r:
                for k in range(RG):
                    pass_on(r, k, True)
                    load((r + 1) * RG + k, ((r + 1) % 2) * RG + k, k)
            r = ROUNDS - 2
            for k in range(RG):
                pass_on(r, k, True)
                slot = ((r + 1) % 2) * RG + k
                if k < RG - 1:
                    load((r + 1) * RG + k, slot, k)
                else:
                    last = feed_g[:, slot, :].rearrange("p (u r) -> p u r", r=ROW)
                    sp.dma_start(last[:, 0:LAST_FULL, 0:FEAT],
                                 edge_cols[:, COLS - LAST_FULL:COLS, :]).then_inc(load_sem[k], 16)
                    sp.wait_ge(load_sem[k], 16 * (r + 2))
                    sp.dma_start(last[0:TAIL, LAST_FULL, 0:FEAT], edge_attr[COLS * P:EDGES, :]).then_inc(load_sem[k], 16)
            for k in range(RG):
                sp.wait_ge(load_sem[k], 16 * (ROUNDS + (k == RG - 1)))
                sp.sem_inc(landed, 1)

            for k in range(RG):
                sp.wait_ge(scattered[k], 16 * GT * ROUNDS)
            sp.wait_ge(self_saved, 16)
            sp.dma_start(feed[:, 0:WINDOWS * ROW], self_part).then_inc(final_loaded, 16)
            for dst, part in x_windows(fin_x):
                sp.dma_start(dst, part).then_inc(final_loaded, 16)

            out_w = out[0:(WINDOWS - 1) * P, :].rearrange("(w p) f -> p w f", p=P)
            for i in range(WINDOWS // RG):
                sp.wait_ge(result_done, RG * (i + 1))
                n = RG if i < WINDOWS // RG - 1 else RG - 1
                sp.dma_start(out_w[:, RG * i:RG * i + n, :], fin_x[:, RG * i:RG * i + n, 0:FEAT]).then_inc(stored, 16)
            sp.dma_start(out[(WINDOWS - 1) * P:NODES, :], fin_x[0:LAST_ROWS, WINDOWS - 1, 0:FEAT]).then_inc(stored, 16)
            sp.wait_ge(stored, 16 * (WINDOWS // RG + 1))

        @block.gpsimd
        def _(pool):
            pool.memset(src_row[:, COLS:TILES], WINDOWS * P).then_inc(pool_set, 1)
            pool.iota(bucket_no[:, :], [[1, BUCKETS]], base=0, channel_multiplier=0,
                      allow_small_or_imprecise_dtypes=True).then_inc(pool_set, 1)
            pool.iota(bucket_col[:, :], [[1, 1]], base=0, channel_multiplier=1,
                      allow_small_or_imprecise_dtypes=True).then_inc(pool_set, 1)
            pool.iota(pair_no[:, :], [[1, MAXT + RT]], base=0, channel_multiplier=0,
                      allow_small_or_imprecise_dtypes=True).then_inc(pool_set, 1)
            pool.memset(below[:, :], 1.0).then_inc(pool_set, 1)
            pool.memset(above[:, :], 1.0).then_inc(pool_set, 1)
            pool.memset(ident[:, :], 0.0).then_inc(pool_set, 1)
            pool.memset(ones_bf[:, :], 1.0).then_inc(pool_set, 1)
            pool.memset(ones_row, 1.0).then_inc(pool_set, 1)
            pool.memset(ends[:, :], 0.0).then_inc(pool_set, 1)
            pool.memset(eps_col[:, :], EPS).then_inc(pool_set, 1)
            pool.wait_ge(pool_set, 11)
            pool.affine_select(out=below[:, :], in_=below[:, :], compare_op=ALU.is_gt, fill=0.0, base=0,
                               pattern=[[1, P]], channel_multiplier=-1).then_inc(pool_set, 1)
            pool.affine_select(out=above[:, :], in_=above[:, :], compare_op=ALU.is_gt, fill=0.0, base=0,
                               pattern=[[-1, P]], channel_multiplier=1).then_inc(pool_set, 1)
            pool.affine_select(out=ident[:, :], in_=ident[:, :], compare_op=ALU.not_equal, fill=1.0, base=0,
                               pattern=[[-1, P]], channel_multiplier=1).then_inc(pool_set, 1)
            tags = feed[:, :].rearrange("p (n r) -> p n r", r=ROW)
            pool.memset(tags[:, :, FEAT:ROW], 1.0).then_inc(pool_set, 1)
            pool.memset(acc_w[:, WINDOWS - 1, 0:FEAT], 0.0).then_inc(pool_set, 1)
            pool.memset(acc_w[:, :, FEAT:ROW], 0.0).then_inc(pool_set, 1)
            pool.iota(node_id[:, :], [[P, BUCKETS], [1, ROW]], base=0, channel_multiplier=0,
                      allow_small_or_imprecise_dtypes=True).then_inc(pool_set, 1)

            with pool.Fori(0, ROUNDS // 2) as i:
                for half_ in range(2):
                    for k in range(RG):
                        slot = half_ * RG + k
                        pool.wait_ge(fed, (2 * i + half_) * RG + k + 1)
                        pool.wait_ge(scattered[k], (2 * i + half_) * (16 * GT))
                        pool.sem_inc(released, 1)
                        for u in range(GT):
                            n = slot * GT + u
                            pool.indirect_dma_start(
                                out=ordered, out_offset=bass.IndirectOffsetOnAxis(ap=dest[:, n:n + 1], axis=0),
                                in_=feed[:, n * ROW:(n + 1) * ROW], in_offset=None,
                            ).then_inc(scattered[k], 16)

        @block.scalar
        def _(act):
            act.dma_start(a_sb, a).then_inc(a_loaded, 16)
            act.dma_start(a2_row, a_2).then_inc(a_loaded, 16)
            act.wait_ge(pool_set, 17)
            for dst, part in x_windows(acc_w):
                act.dma_start(dst, part).then_inc(x_loaded, 16)
            act.wait_ge(weights_step, 1)
            act.copy(A1T[:, :], bank(6, 0, P)).then_inc(weights_copied, 1)
            act.copy(A2T[:, :], bank(6, P, P)).then_inc(weights_copied, 1)
            act.copy(a2_wide, bank(6, 2 * P, P)).then_inc(weights_copied, 1)
            act.wait_ge(weights_step, 2)
            act.copy(node_w[:, :], bank(7, 0, P)).then_inc(weights_copied, 1)
            act.copy(edge_w[:, :], bank(7, P, P)).then_inc(weights_copied, 1)
            act.wait_ge(var_done, 1)
            act.activation(rstd[:, :], moments[:, :, 1], ACT.Sqrt, bias=eps_col[:, :]).then_inc(std_done, 1)
            act.wait_ge(norm_done, 1)

            def node_window(w, k):
                b = k % 2
                xw = acc[:, bass.ds(w * ROW, FEAT)]
                act.activation(h_st[:, b, :], xw, ACT.Relu, bias=shift_n[:, bass.ds(w, 1)],
                               scale=rstd[:, bass.ds(w, 1)]).then_inc(h_done, 1)
                act.wait_ge(hT_done, w + 1)
                act.copy(hT_st[:, b, :], bank(6 + b, 0, P)).then_inc(hT_copied, 1)
                act.wait_ge(self_done, w + 1)
                act.copy(node_score[:, bass.ds(w * ROW, P)], bank(6 + b, P, P)).then_inc(self_copied, 1)
                act.copy(xw, bank(6 + b, 2 * P, P)).then_inc(self_copied, 1)

            with act.Fori(0, WINDOWS // RG) as i:
                for k in range(RG):
                    node_window(RG * i + k, k)
            act.mul(node_score[:, WINDOWS * ROW:BUCKETS * ROW], ident[:, 0:1].to_broadcast([P, ROW]), 0.0)\
               .then_inc(self_copied, 1)
            act.wait_ge(self_copied, 2 * WINDOWS + 1)
            act.dma_start(self_part, acc[:, 0:WINDOWS * ROW]).then_inc(self_saved, 16)

            def read_back(c, r, k):
                g = (FIRST[c] + r) * RG + k
                act.dma_start(back_g[:, bass.ds(((FIRST[c] + r) % 2) * RG + k, 1), :],
                              ordered_g[bass.ds(g, 1), :, :].rearrange("g p r -> p g r")).then_inc(back_sem[k], 16)

            def step(c, r, k, fetch):
                S = (STEP_ROUND[c] + r) * RG + k
                slots = load_pairs(ENGINE.Activation, S, 1)
                wins = load_pairs(ENGINE.Activation, S, 0)
                if fetch is not None:
                    if not isinstance(S, int) or S >= 2:
                        act.wait_ge(product_done, GT * (S - 1))
                    read_back(c, *fetch)
                if r is not CHUNKS[c]:
                    act.wait_ge(back_sem[k], 16 * (FIRST[c] + r + 1))
                later = not isinstance(S, int) or S > 0
                for u in range(GT):
                    if later:
                        act.wait_ge(weighted_done, GT * (S - 1) + u + 1)
                    act.activation(dist[:, u, :], node_id[:, bass.ds(wins[u], P)], ACT.Abs, scale=-1.0,
                                   bias=back[:, bass.ds(slots[u] + SRC, 1)]).then_inc(dist_done, 1)
                act.wait_ge(leaky_done, S + 1)
                if later:
                    act.wait_ge(weighted_done, GT * S)
                act.activation(prob[:, 0, :], neg_leaky[:, 0, :], ACT.Exp, scale=-1.0).then_inc(prob_done, 1)
                act.wait_ge(prob_done, 2 * S + 1)
                act.mul(neg_prob[:, 0, :], prob[:, 0, :], -1.0).then_inc(prob_done, 1)
                act.wait_ge(prob_done, 2 * S + 2)
                act.wait_ge(dist_done, GT * (S + 1))
                for u in range(GT):
                    n = (k * GT + u) % WRING
                    if not isinstance(S, int) or GT * S + u >= WRING:
                        act.wait_ge(product_done, GT * S + u + 1 - WRING)
                    act.activation(weighted[:, n, :], dist[:, u, :], ACT.Relu, bias=prob[:, 0, u:u + 1],
                                   scale=neg_prob[:, 0, u:u + 1]).then_inc(weighted_done, 1)

            act.wait_ge(pool_set, 18)
            for c, rounds in enumerate(CHUNKS):
                if c == 0:
                    act.wait_ge(table_done, len(CHUNKS))
                    act.wait_ge(acc_zero, 1)
                for k in range(RG):
                    act.wait_ge(scattered[k], 16 * GT * (FIRST[c] + rounds))
                if c:
                    act.wait_ge(product_done, GT * STEP_ROUND[c] * RG)
                for k in range(5):
                    read_back(c, 0, k)
                r0 = 0
                if c == 0:
                    for k in range(RG):
                        step(c, 0, k, (0, k + 5) if k < 2 else (1, k - 2))
                    r0 = 1
                if r0 < rounds - 1:
                    with act.Fori(r0, rounds - 1) as r:
                        for k in range(RG):
                            step(c, r, k, (r, k + 5) if k < 2 else (r + 1, k - 2))
                for k in range(RG):
                    step(c, rounds - 1, k, (rounds - 1, k + 5) if k < 2 else None)
                for k in range(RG):
                    step(c, rounds, k, None)

            with act.Fori(0, WINDOWS // RG) as i:
                for k in range(RG):
                    act.wait_ge(scaledT_done, RG * i + k + 1)
                    act.copy(scaledT[:, k, :], bank(k, 0, P)).then_inc(scaledT_copied, 1)

        @block.tensor
        def _(pe):
            pe.wait_ge(a_loaded, 32)
            pe.wait_ge(pool_set, 14)
            pe.transpose(bank(6, 0, P), a_sb[:, 0:FEAT], ident[:, :])
            pe.transpose(bank(6, P, P), a_sb[:, FEAT:2 * FEAT], ident[:, :])
            pe.matmul(bank(6, 2 * P, P), a2_row, ones_row, start=True, stop=True).then_inc(weights_step, 1)
            pe.wait_ge(weights_copied, 3)
            pe.matmul(bank(7, 0, P), a_sb[:, 0:FEAT], a2_wide, start=True, stop=True)
            pe.matmul(bank(7, P, P), a2_wide, a_sb[:, FEAT:2 * FEAT], start=True, stop=True).then_inc(weights_step, 1)

            def rank_sums(c):
                tiles = CHUNKS[c] * RT
                pe.wait_ge(ends_done, c + 1)
                pe.matmul(bank(0, 0, BUCKETS), below[:, :], ends[:, 1:BUCKETS + 1], start=True, stop=False)
                pe.matmul(bank(0, 0, BUCKETS), above[:, :], ends[:, 0:BUCKETS], start=False, stop=True)
                pe.matmul(bank(1, 0, 1, BUCKETS), ends[:, 0:BUCKETS], ones_bf[:, :], start=True, stop=True)\
                  .then_inc(shift_done, 1)
                pe.wait_ge(started_done, c + 1)
                pe.matmul(bank(2, 0, tiles + RT, 1), ones_bf[0:BUCKETS, :], started[:, 0:tiles + RT],
                          start=True, stop=True).then_inc(pairs_done, 1)

            for c in range(len(CHUNKS)):
                rank_sums(c)

            pe.wait_ge(weights_copied, 5)

            def node_window(w, k):
                b = k % 2
                pe.wait_ge(h_done, w + 1)
                pe.transpose(bank(6 + b, 0, P), h_st[:, b, :], ident[:, :]).then_inc(hT_done, 1)
                pe.wait_ge(hT_copied, w + 1)
                pe.matmul(bank(6 + b, P, P), node_w[:, :], hT_st[:, b, :], start=True, stop=True)
                pe.matmul(bank(6 + b, 2 * P, P), hT_st[:, b, :], A1T[:, :], start=True, stop=True)\
                  .then_inc(self_done, 1)

            with pe.Fori(0, WINDOWS // RG) as i:
                for k in range(RG):
                    node_window(RG * i + k, k)

            def step(S, k, first=False):
                slots = load_pairs(ENGINE.PE, S, 1)
                for u in range(GT):
                    n = (k * GT + u) % WRING
                    pe.wait_ge(weighted_done, GT * S + u + 1)
                    if u % PER_BANK == 0 and not first:
                        pe.wait_ge(acc_done, GT * (S - 2) + min(u + PER_BANK, GT))
                    dst = psum[:, bass.ds((S % 2) * (3 * 512) + (u // PER_BANK) * 512 + (u % PER_BANK) * (FEAT + 1),
                                          FEAT + 1)]
                    pe.matmul(dst, weighted[:, n, :], back[:, bass.ds(slots[u], FEAT + 1)],
                              start=True, stop=True).then_inc(product_done, 1)

            pe.wait_ge(table_done, len(CHUNKS))
            for k in range(RG):
                step(k, k, first=k < 2)
            with pe.Fori(1, STEP_ROUNDS) as r:
                for k in range(RG):
                    step(r * RG + k, k)

            pe.wait_ge(acc_done, GT * STEPS)
            with pe.Fori(0, WINDOWS // RG) as i:
                for k in range(RG):
                    pe.wait_ge(scaled_done, RG * i + k + 1)
                    pe.transpose(bank(k, 0, P), scaled[:, k, :], ident[:, :]).then_inc(scaledT_done, 1)
                for k in range(RG):
                    pe.wait_ge(scaledT_copied, RG * i + k + 1)
                    pe.matmul(bank(k, P, P), scaledT[:, k, :], A2T[:, :], start=True, stop=True).then_inc(out_ready, 1)

        @block.vector
        def _(dve):
            made = [0]

            def done(ins):
                made[0] += 1
                ins.then_inc(vec, 1)
                dve.wait_ge(vec, made[0])

            dve.wait_ge(src_loaded, 32)
            dve.wait_ge(pool_set, 11)
            dve.tensor_copy(src16[:, :], src_row[:, :]).then_inc(vec, 1)
            tmp = picked[:, 0:TILES].bitcast(I32)
            dve.tensor_scalar(tmp, src_row[:, :], 7, None, ALU.arith_shift_right).then_inc(vec, 1)
            dve.wait_ge(vec, 2)
            made[0] = 2
            done(dve.tensor_copy(bucket[:, :], tmp))

            def rank_chunk(c):
                t0, tiles = FIRST[c] * RT, CHUNKS[c] * RT
                n0 = made[0]
                with dve.Fori(0, BUCKETS // BB) as i:
                    for k in range(BB):
                        dve.tensor_scalar(hot[:, bass.ds((i * BB + k) * tiles, tiles)], bucket[:, t0:t0 + tiles],
                                          bucket_no[:, bass.ds(i * BB + k, 1)], None, ALU.is_equal)\
                           .then_inc(hots_done, 1)
                dve.wait_ge(hots_done, BUCKETS * (c + 1))
                flat = BUCKETS * tiles
                done(dve.tensor_tensor_scan(count[:, 0:flat], hot[:, 0:flat], hot[:, 0:flat], 0.0, ALU.add, ALU.max))
                by_bucket = count[:, 0:flat].rearrange("p (b t) -> p b t", t=tiles)
                done_ends = dve.tensor_copy(ends[:, 1:BUCKETS + 1], by_bucket[:, :, tiles - 1])
                done_ends.then_inc(ends_done, 1)
                dve.wait_ge(shift_done, c + 1)
                done(dve.tensor_scalar(shift[:, :], bank(0, 0, BUCKETS), -1.0, None, ALU.add))
                n0 = made[0]
                with dve.Fori(0, BUCKETS // BB) as i:
                    for k in range(BB):
                        at = bass.ds((i * BB + k) * tiles, tiles)
                        dve.scalar_tensor_tensor(out=picked[:, k * tiles:(k + 1) * tiles], in0=count[:, at],
                                                 scalar=shift[:, bass.ds(i * BB + k, 1)], in1=hot[:, at],
                                                 op0=ALU.add, op1=ALU.mult).then_inc(vec, 1)
                    dve.wait_ge(vec, n0 + (BB + 1) * i + BB)
                    dve.tensor_reduce(partial[:, bass.ds(i * tiles, tiles)],
                                      picked[:, 0:BB * tiles].rearrange("p (b t) -> p t b", t=tiles),
                                      AX_X, ALU.add).then_inc(vec, 1)
                    dve.wait_ge(vec, n0 + (BB + 1) * (i + 1))
                made[0] = n0 + (BB + 1) * (BUCKETS // BB)
                rk = rank[:, 0:tiles]
                done(dve.tensor_reduce(rk, partial[:, 0:5 * tiles].rearrange("p (b t) -> p t b", t=tiles),
                                       AX_X, ALU.add))
                ri, pa, pb, pc = (v[:, 0:tiles] for v in (rank_i, part_a, part_b, part_c))
                done(dve.tensor_copy(ri, rk))
                low, mid = (P - 1).bit_length(), (GT - 1).bit_length()
                dve.tensor_scalar(pa, ri, low + mid, low + mid, ALU.arith_shift_right, ALU.logical_shift_left)\
                   .then_inc(vec, 1)
                dve.tensor_scalar(pb, ri, P - 1, mid, ALU.bitwise_and, ALU.logical_shift_left).then_inc(vec, 1)
                dve.tensor_scalar(pc, ri, low, GT - 1, ALU.arith_shift_right, ALU.bitwise_and).then_inc(vec, 1)
                made[0] += 3
                dve.wait_ge(vec, made[0])
                done(dve.tensor_tensor(pa, pa, pb, ALU.bitwise_or))
                done(dve.tensor_tensor(pa, pa, pc, ALU.bitwise_or))
                done(dve.tensor_scalar(src_row[:, t0:t0 + tiles], pa, float(FIRST[c] * RT * P), None, ALU.add))

                npairs = tiles + RT
                fp = first_pair
                done(dve.tensor_copy(first_pair_i[:, :], bank(1, 0, 1, BUCKETS)))
                done(dve.tensor_scalar(first_pair_i[:, :], first_pair_i[:, :], low, None, ALU.arith_shift_right))
                done(dve.tensor_copy(fp[:, 0:1], first_pair_i[:, :]))
                done(dve.tensor_scalar(fp[:, 1:2], fp[:, 0:1], float(tiles - 1), bucket_col[:, :], ALU.min, ALU.add))
                dve.tensor_scalar(started[:, 0:npairs], pair_no[:, 0:npairs], fp[:, 1:2], None, ALU.is_ge)\
                   .then_inc(started_done, 1)
                dve.wait_ge(pairs_done, c + 1)
                win, tile, wrap = (v[:, 0:npairs] for v in (row1, row2, row3))
                done(dve.tensor_scalar(win, bank(2, 0, npairs, 1), -1.0, None, ALU.add))
                done(dve.tensor_tensor(tile, pair_no[0:1, 0:npairs], win, ALU.subtract))
                done(dve.tensor_scalar(tile, tile, float(tiles - 1), float((FIRST[c] % 2) * RT), ALU.min, ALU.add))
                for _ in range((MAXT + RT) // (SLOTS * GT)):
                    done(dve.tensor_scalar(wrap, tile, float(SLOTS * GT), float(-SLOTS * GT), ALU.is_ge, ALU.mult))
                    done(dve.tensor_tensor(tile, tile, wrap, ALU.add))
                s0 = STEP_ROUND[c] * RG
                tab = table[:, s0 * TSTEP:(s0 + npairs // GT) * TSTEP].rearrange("q (s n) -> q s n", n=TSTEP)
                dve.tensor_scalar(tab[:, :, 0:GT], win.rearrange("q (s n) -> q s n", n=GT), float(ROW), None,
                                  ALU.mult).then_inc(vec, 1)
                made[0] += 1
                dve.tensor_scalar(tab[:, :, GT:TSTEP], tile.rearrange("q (s n) -> q s n", n=GT), float(ROW), None,
                                  ALU.mult).then_inc(table_done, 1)
                dve.wait_ge(vec, made[0])
                dve.wait_ge(table_done, c + 1)

            fed_groups = [0]

            def feed_rounds(r0, rounds):
                if r0 == 0:
                    dve.wait_ge(pool_set, 15)
                    dve.wait_ge(weights_copied, 5)
                with dve.Fori(r0 * RG, (r0 + rounds) * RG) as g:
                    slot = g % SLOTS
                    dve.wait_ge(landed, g + 1)
                    dve.wait_ge(edge_dots, g * GT)
                    for u in range(GT):
                        if u >= JUNK:
                            dve.wait_ge(edge_dots, g * GT + u + 1 - JUNK)
                        dve.scalar_tensor_tensor(out=junk[:, u % JUNK, :], in0=feed[:, bass.ds((slot * GT + u) * ROW, FEAT)],
                                                 scalar=1.0, in1=edge_w[:, :], op0=ALU.mult, op1=ALU.mult,
                                                 accum_out=feed[:, bass.ds((slot * GT + u) * ROW + SCORE, 1)])\
                           .then_inc(edge_dots, 1)
                    tags = feed_g[:, bass.ds(slot, 1), :].rearrange("p g (u r) -> p (g u) r", r=ROW)
                    dve.tensor_copy(tags[:, :, SRC], src16[:, bass.ds(g * GT, GT)])
                    dve.tensor_copy(dest[:, bass.ds(slot * GT, GT)], src_row[:, bass.ds(g * GT, GT)]).then_inc(fed, 1)

            def norm():
                dve.wait_ge(x_loaded, 32)
                dve.wait_ge(pool_set, 17)
                with dve.Fori(0, WINDOWS) as w:
                    dve.bn_stats(stats[:, bass.ds(w * 6, 6)], acc[:, bass.ds(w * ROW, FEAT)]).then_inc(stats_done, 1)
                dve.wait_ge(stats_done, WINDOWS)
                both = stats.rearrange("p (w s) -> p w s", s=6)
                mean, var, half_gap = moments[:, :, 0], moments[:, :, 1], kept[:, :]
                dve.tensor_tensor(mean, both[:, :, 1], both[:, :, 4], ALU.add).then_inc(vec, 1)
                dve.tensor_tensor(half_gap, both[:, :, 1], both[:, :, 4], ALU.subtract).then_inc(vec, 1)
                dve.tensor_tensor(var, both[:, :, 2], both[:, :, 5], ALU.add).then_inc(vec, 1)
                made[0] += 3
                dve.wait_ge(vec, made[0])
                done(dve.tensor_scalar(mean, mean, 0.5, None, ALU.mult))
                done(dve.tensor_scalar(half_gap, half_gap, 0.5, None, ALU.mult))
                done(dve.tensor_tensor(half_gap, half_gap, half_gap, ALU.mult))
                dve.scalar_tensor_tensor(out=var, in0=var, scalar=1.0 / FEAT, in1=half_gap, op0=ALU.mult,
                                         op1=ALU.add).then_inc(var_done, 1)
                dve.wait_ge(std_done, 1)
                done(dve.reciprocal(rstd[:, :], rstd[:, :]))
                dve.scalar_tensor_tensor(out=shift_n[:, :], in0=moments[:, :, 0], scalar=-1.0, in1=rstd[:, :],
                                         op0=ALU.mult, op1=ALU.mult).then_inc(norm_done, 1)

            def add_pair(S, u, wins, first=False):
                if u % PER_BANK == 0:
                    dve.wait_ge(product_done, GT * S + min(u + PER_BANK, GT))
                if not first:
                    dve.wait_ge(acc_done, GT * S + u)
                at = (S % 2) * (3 * 512) + (u // PER_BANK) * 512 + (u % PER_BANK) * (FEAT + 1)
                sums = acc[:, bass.ds(wins[u], FEAT + 1)]
                dve.tensor_tensor(sums, sums, psum[:, bass.ds(at, FEAT + 1)], ALU.add).then_inc(acc_done, 1)

            def step(c, r, k, lag=True):
                S = (STEP_ROUND[c] + r) * RG + k
                wins = load_pairs(ENGINE.DVE, S, 0)
                slots = load_pairs(ENGINE.DVE, S, 1)
                old = load_pairs(ENGINE.DVE, S - 2, 0) if lag else None
                if r is not CHUNKS[c]:
                    dve.wait_ge(back_sem[k], 16 * (FIRST[c] + r + 1))
                first = isinstance(S, int) and S == 2
                if not (isinstance(S, int) and S == 0):
                    dve.wait_ge(node_sums, GT * S)
                    dve.wait_ge(z_done, GT * S)
                for u in range(GT):
                    if u >= JUNK:
                        dve.wait_ge(node_sums, GT * S + u + 1 - JUNK)
                    dve.scalar_tensor_tensor(out=junk2[:, u % JUNK, :], in0=node_id[:, bass.ds(wins[u], P)],
                                             scalar=back[:, bass.ds(slots[u] + SRC, 1)],
                                             in1=node_score[:, bass.ds(wins[u], P)],
                                             op0=ALU.is_equal, op1=ALU.mult,
                                             accum_out=zsum[:, 0, u:u + 1]).then_inc(node_sums, 1)
                    if lag and u < GT // 2:
                        add_pair(S - 2, u, old, first and u == 0)
                dve.wait_ge(node_sums, GT * (S + 1))
                if not (isinstance(S, int) and S == 0):
                    dve.wait_ge(leaky_done, S)
                for u in range(GT):
                    dve.tensor_tensor(zed[:, 0, u:u + 1], zsum[:, 0, u:u + 1],
                                      back[:, bass.ds(slots[u] + SCORE, 1)], ALU.add).then_inc(z_done, 1)
                if lag:
                    add_pair(S - 2, GT // 2, old)
                dve.wait_ge(z_done, GT * (S + 1))
                if not (isinstance(S, int) and S == 0):
                    dve.wait_ge(prob_done, 2 * S)
                dve.scalar_tensor_tensor(out=neg_leaky[:, 0, :], in0=zed[:, 0, :], scalar=SLOPE, in1=zed[:, 0, :],
                                         op0=ALU.mult, op1=ALU.max).then_inc(leaky_done, 1)
                if lag:
                    for u in range(GT // 2 + 1, GT):
                        add_pair(S - 2, u, old)

            def pair_rounds(c, r0, r1):
                n = CHUNKS[c]
                if c == 0 and r0 == 0:
                    dve.wait_ge(self_saved, 16)
                    dve.wait_ge(pool_set, 18)
                    dve.memset(acc[:, :], 0.0).then_inc(acc_zero, 1)
                    dve.wait_ge(acc_zero, 1)
                    dve.wait_ge(self_copied, 2 * WINDOWS + 1)
                    for k in range(RG):
                        step(0, 0, k, lag=k >= 2)
                    r0 = 1
                if r0 < min(n, r1):
                    with dve.Fori(r0, min(n, r1)) as r:
                        for k in range(RG):
                            step(c, r, k)
                if r1 > n:
                    for k in range(RG):
                        step(c, n, k)

            place = [0] * len(CHUNKS)
            for what, *at in PLAN:
                if what == "rank":
                    rank_chunk(at[0])
                elif what == "feed":
                    feed_rounds(*at)
                elif what == "norm":
                    norm()
                else:
                    c = at[0]
                    end = at[1] if len(at) > 1 else CHUNKS[c] + 1
                    pair_rounds(c, place[c], end)
                    place[c] = end
            assert place == [n + 1 for n in CHUNKS]
            for S in (STEPS - 2, STEPS - 1):
                wins = load_pairs(ENGINE.DVE, S, 0)
                for u in range(GT):
                    add_pair(S, u, wins)

            dve.wait_ge(acc_done, GT * STEPS)
            total = acc_w[:, 0:WINDOWS, ONE]
            done(dve.tensor_scalar(denom[:, :], total, 0.0, TINY, ALU.is_equal, ALU.mult))
            done(dve.tensor_tensor(denom[:, :], denom[:, :], total, ALU.add))
            done(dve.reciprocal(inv[:, :], denom[:, :]))
            done(dve.tensor_tensor(kept[:, :], total, inv[:, :], ALU.mult))
            dve.wait_ge(final_loaded, 48)

            n0 = made[0]
            with dve.Fori(0, WINDOWS // RG) as i:
                for k in range(RG):
                    w = RG * i + k
                    dve.tensor_scalar(scaled[:, k, :], acc[:, bass.ds(w * ROW, FEAT)], inv[:, bass.ds(w, 1)], None,
                                      ALU.mult).then_inc(scaled_done, 1)
                for k in range(RG):
                    w = RG * i + k
                    xw = feed[:, bass.ds((WINDOWS + w) * ROW, FEAT)]
                    dve.scalar_tensor_tensor(out=xw, in0=feed[:, bass.ds(w * ROW, FEAT)],
                                             scalar=kept[:, bass.ds(w, 1)], in1=xw, op0=ALU.mult,
                                             op1=ALU.add).then_inc(self_added, 1)
                for k in range(RG):
                    w = RG * i + k
                    xw = feed[:, bass.ds((WINDOWS + w) * ROW, FEAT)]
                    dve.wait_ge(out_ready, w + 1)
                    dve.wait_ge(self_added, w + 1)
                    dve.tensor_tensor(xw, xw, bank(k, P, P), ALU.add).then_inc(result_done, 1)


_INS = [("x", F32), ("src", I32), ("edge_attr_128", F32), ("L0_gnn_a", F32), ("L0_gnn_a_2", F32)]


def kernel(x, src, dst, edge_attr_128, L0_gnn_a, L0_gnn_a_2):
    import concourse.bacc as bacc
    from concourse.bass_utils import run_bass_kernel_spmd

    nc = bacc.Bacc("TRN2", target_bir_lowering=False, num_devices=1, dynamic_dma_scratch_size=8192)
    given = {"x": x, "src": src, "edge_attr_128": edge_attr_128, "L0_gnn_a": L0_gnn_a, "L0_gnn_a_2": L0_gnn_a_2}
    arrays, args = {}, []
    for name, dt in _INS:
        arr = np.ascontiguousarray(given[name])
        arrays[f"in_{name}"] = arr
        args.append(nc.dram_tensor(f"in_{name}", arr.shape, dt, kind="ExternalInput").ap())
    args.append(nc.dram_tensor("out_0", (NODES, FEAT), F32, kind="ExternalOutput").ap())
    gnn_kernel(nc, *args)
    r = run_bass_kernel_spmd(nc, [arrays], core_ids=[0])
    return r.results[0]["out_0"]
```

```python
from contextlib import ExitStack

import numpy as np

import concourse.bass as bass
from concourse import mybir

ALU = mybir.AluOpType
ACT = mybir.ActivationFunctionType
F32 = mybir.dt.float32
BF16 = mybir.dt.bfloat16
I16 = mybir.dt.int16
I32 = mybir.dt.int32
U32 = mybir.dt.uint32
AX_X = mybir.AxisListType.X
ENGINE = mybir.EngineType

P = 128
NODES, EDGES, FEAT = 6250, 100000, 128
EPS = 1e-5
SLOPE = 0.2
TINY = 1e-12

WINDOWS = -(-NODES // P)
BUCKETS = WINDOWS + 1
LAST_ROWS = NODES - (WINDOWS - 1) * P

COLS = EDGES // P
TAIL = EDGES - COLS * P
GT = 8
RG = 7
RT = GT * RG
ROUNDS = -(-(COLS + 1) // RT)
TILES = ROUNDS * RT
GROUPS = ROUNDS * RG
LAST_FULL = COLS - (GROUPS - 1) * GT

CHUNKS = [2, 4, 4, 2, 2]
assert sum(CHUNKS) == ROUNDS and RT >= BUCKETS - 1
FIRST = [sum(CHUNKS[:c]) for c in range(len(CHUNKS))]
STEP_ROUND = [FIRST[c] + c for c in range(len(CHUNKS))]
STEP_ROUNDS = ROUNDS + len(CHUNKS)
STEPS = STEP_ROUNDS * RG
MAXT = max(CHUNKS) * RT

SLOTS = 2 * RG
ROW = FEAT + 4
PROB, SRC = FEAT, FEAT + 1
SPAN = 9
ACT_PAIRS = 4
BB = 10
JUNK = 4
PER_BANK = 3
NO_CHECK = "the table's entries are clamped on chip"

FETCH = 5
AHEAD = 4
BLOCKS = -(-TILES // P)

PLAN = [
    ("count", 0), ("rank", 0), ("nodes",), ("feed", 0, 1), ("feed", 1, 1), ("feed", 2, 12),
    ("count", 1), ("rank", 1), ("feed", 14, 12), ("count", 2), ("feed", 26, 4), ("rank", 2),
    ("feed", 30, 5), ("count", 3), ("rank", 3), ("feed", 35, 7), ("count", 4), ("rank", 4),
    ("pairs", 0, 0, 3, 42, 4), ("pairs", 1, 0, 5, 54, 4), ("pairs", 2, 0, 5, 74, 4),
    ("pairs", 3, 0, 1, 94, 4), ("pairs", 3, 1, 3, 98, 0), ("pairs", 4, 0, 3, 98, 0),
]


def stretches(c, r0, r1):
    cuts = {r0, r1} | {r for r in (CHUNKS[c] - 1, CHUNKS[c]) if r0 < r < r1}
    if c == 0 and r0 == 0:
        cuts.add(1)
    cuts = sorted(cuts)
    return list(zip(cuts, cuts[1:]))


def run_feeds(engine, g0, n, feed_group):
    if n == 1:
        feed_group(g0)
    else:
        with engine.Fori(g0, g0 + n) as g:
            feed_group(g)


def run_pairs(engine, c, r0, r1, g0, per, step, feed_group):
    after = {(j + 1) * RG // per - 1: j for j in range(per)}
    for lo, hi in stretches(c, r0, r1):
        def body(r):
            for k in range(RG):
                step(c, r, k)
                if k in after:
                    feed_group(g0 - per * r0 + per * r + after[k])
        if hi - lo == 1:
            body(lo)
        else:
            with engine.Fori(lo, hi) as r:
                body(r)


def hot_buffer(k):
    return 2 if k == RG - 1 else k % 2


def gnn_kernel(nc, x, src, edge_attr, a, a_2, out):
    ctx = ExitStack()
    with ctx:
        def sb(name, shape, dt):
            return ctx.enter_context(nc.sbuf_tensor(name, shape, dt))

        def sem(name):
            return ctx.enter_context(nc.semaphore(name))

        ordered = nc.dram_tensor("ordered_rows", [TILES * P, ROW], F32, kind="Internal").ap()
        self_part = nc.dram_tensor("self_part", [P, WINDOWS * ROW], F32, kind="Internal").ap()
        places = nc.dram_tensor("places", [TILES, P], BF16, kind="Internal").ap()

        feed = sb("feed", [P, SLOTS * GT * ROW], F32)
        back = sb("back", [P, SLOTS * GT * ROW], F32)
        acc = sb("acc", [P, (BUCKETS + SPAN - 1) * ROW], F32)
        node_id = sb("node_id", [P, BUCKETS * ROW], I16)
        table = sb("table", [65, STEPS * GT], I32)
        hots = sb("hots", [P, 3 * GT, P], F32)
        dist = sb("dist", [P, ACT_PAIRS, P], BF16)
        place_rows = sb("place_rows", [P, RG, GT * P], BF16)
        place_hot = sb("place_hot", [P, GT * P], BF16)
        window = sb("window", [P, GT], F32)
        chosen = sb("chosen", [P, GT, BUCKETS], F32)
        score_parts = sb("score_parts", [P, 3, BUCKETS], BF16)
        score_rest = sb("score_rest", [P, BUCKETS], F32)
        src_row = sb("src_row", [P, TILES], I32)
        src16 = sb("src16", [P, TILES], I16)
        bucket = sb("bucket", [P, TILES], BF16)
        dest = sb("dest", [P, SLOTS * GT], U32)
        junk = sb("junk", [P, JUNK, P], F32)
        edge_w = sb("edge_w", [P, FEAT], F32)
        A2T = sb("A2T", [P, FEAT], F32)
        A1w = sb("A1w", [P, FEAT + 1], F32)
        ident = sb("ident", [P, P], F32)
        ident_bf = sb("ident_bf", [P, P], BF16)
        below = sb("below", [P, P], BF16)
        above = sb("above", [P, P], BF16)
        ones_bf = sb("ones_bf", [P, P], BF16)
        zeros = sb("zeros", [1, PER_BANK * (FEAT + 1)], BF16)
        lane = sb("lane", [P, 1], F32)
        bucket_no = sb("bucket_no", [P, BUCKETS], F32)
        ends = sb("ends", [P, BUCKETS + 1], BF16)
        shift = sb("shift", [P, BUCKETS], F32)
        first_pair = sb("first_pair", [BUCKETS, 2], F32)
        first_pair_i = sb("first_pair_i", [BUCKETS, 1], I32)
        edge_score = sb("edge_score", [P, GT], F32)
        node_part = sb("node_part", [P, GT], F32)
        zed = sb("zed", [P, GT], F32)
        leaky = sb("leaky", [P, 2, GT], F32)
        moments = sb("moments", [P, WINDOWS, 2], F32)
        eps_col = sb("eps_col", [P, 1], F32)
        rstd = sb("rstd", [P, WINDOWS], F32)
        denom = sb("denom", [P, WINDOWS], F32)
        inv = sb("inv", [P, WINDOWS], F32)
        kept = sb("kept", [P, WINDOWS], F32)
        pair_no = sb("pair_no", [P, MAXT + RT], F32)
        psum_set = sb("psum_set", [65, MAXT + RT + GT], F32)

        half = back[:, :].bitcast(BF16)
        hot = half[:, 0:BUCKETS * MAXT]
        count = half[:, BUCKETS * MAXT:2 * BUCKETS * MAXT]
        f0 = BUCKETS * MAXT
        picked = back[:, f0:f0 + BB * MAXT]
        partial = back[:, f0 + BB * MAXT:f0 + (BB + 5) * MAXT]
        rank = back[:, f0 + (BB + 5) * MAXT:f0 + (BB + 6) * MAXT]
        assert f0 + (BB + 6) * MAXT <= SLOTS * GT * ROW and BUCKETS == 5 * BB
        rank_i, part_a, part_b, part_c = (picked[:, n * MAXT:(n + 1) * MAXT].bitcast(I32) for n in range(4))
        row_win, row_tile, row_wrap = (picked[0:65, n * MAXT:(n + 2) * MAXT] for n in (4, 6, 8))
        started = partial[0:BUCKETS, 0:MAXT + RT].bitcast(BF16)
        a_sb = hots[:, 14:16, :].rearrange("p c f -> p (c f)")
        a2_row = hots[0:1, 16, :]
        ones_row = hots[0:1, 17, :]
        a2_wide = hots[:, 18, :]
        place_bf = hots[:, 0:RG, :].bitcast(BF16).rearrange("p c f -> p (c f)")[:, 0:TILES]
        placeT = hots[:, 20:24, :].bitcast(BF16).rearrange("p c f -> p (c f)")[:, 0:BLOCKS * P]
        stats = feed[:, (SLOTS * GT - 3) * ROW:(SLOTS * GT - 3) * ROW + 6 * WINDOWS]

        psum = ctx.enter_context(nc.psum_tensor("psum", [P, 8 * 512], F32))
        psum_sets = psum[:, 0:6 * 512].rearrange("p (s b f) -> p s b f", s=2, b=3)
        SCORES, RANKS = 6, 7

        def bank(b, lo, n, rows=P):
            return psum[0:rows, b * 512 + lo:b * 512 + lo + n]

        names = """x_loaded a_loaded src_loaded pool_set released landed fed vec hots_done ends_done shift_done
            started_done pairs_done table_done place_made placeT_done placeT_copied place_stored
            weights_step weights_copied stats_done mean_done var_done std_done rstd_done centred_done
            centredT_done centredT_copied self_done self_copied self_saved parts_done acc_zero
            edge_dots place_hot_done window_copied selected zed_done node_scores leaky_done prob_done tagged act_hot dve_hot dist_done
            step_done acc_done scaled_done scaledT_done scaledT_copied out_ready self_added result_done
            final_loaded stored""".split()
        (x_loaded, a_loaded, src_loaded, pool_set, released, landed, fed, vec, hots_done, ends_done, shift_done,
         started_done, pairs_done, table_done, place_made, placeT_done, placeT_copied, place_stored,
         weights_step, weights_copied, stats_done, mean_done, var_done, std_done, rstd_done, centred_done,
         centredT_done, centredT_copied, self_done, self_copied, self_saved, parts_done, acc_zero,
         edge_dots, place_hot_done, window_copied, selected, zed_done, node_scores, leaky_done, prob_done, tagged, act_hot, dve_hot, dist_done,
         step_done, acc_done, scaled_done, scaledT_done, scaledT_copied, out_ready, self_added, result_done,
         final_loaded, stored) = (sem(n) for n in names)
        load_sem = [sem(f"load{k}") for k in range(RG)]
        place_sem = [sem(f"place{k}") for k in range(RG)]
        scattered = [sem(f"scattered{k}") for k in range(RG)]
        back_sem = [sem(f"back{k}") for k in range(RG)]

        feed_g = feed[:, :].rearrange("p (g r) -> p g r", r=GT * ROW)
        back_g = back[:, :].rearrange("p (g r) -> p g r", r=GT * ROW)
        edge_cols = edge_attr[0:COLS * P, :].rearrange("(p t) f -> p t f", t=COLS)
        ordered_g = ordered.rearrange("(g p u) r -> g p (u r)", p=P, u=GT)
        acc_w = acc[:, :].rearrange("p (w r) -> p w r", r=ROW)

        fin_x = feed[:, WINDOWS * ROW:2 * WINDOWS * ROW].rearrange("p (w r) -> p w r", r=ROW)
        stage = hots[:, 0:RG, :]
        stageT = hots[:, RG:2 * RG, :]

        def x_windows(dst):
            whole = x[0:(WINDOWS - 1) * P, :].rearrange("(w p) f -> p w f", p=P)
            return ((dst[:, 0:WINDOWS - 1, 0:FEAT], whole),
                    (dst[0:LAST_ROWS, WINDOWS - 1, 0:FEAT], x[(WINDOWS - 1) * P:NODES, :]))

        WIN, SLOT, PLACE = 0, 32, 64
        MOST = {WIN: (BUCKETS - 1) * ROW, SLOT: (SLOTS * GT - 1) * ROW, PLACE: 5 * 512 + 2 * (FEAT + 1)}

        def load_pairs(engine, S, what, lo, n):
            got = []
            for at in range(lo, lo + n, 4):
                _, vals = nc.values_load_multi_w_load_instructions(
                    table[what:what + 1, bass.ds(S * GT + at, min(4, lo + n - at))], engines=[engine],
                    min_val=0, max_val=MOST[what], skip_runtime_bounds_check_because=NO_CHECK)
                got += vals
            return got

        def step_no(c, r, k):
            return (STEP_ROUND[c] + r) * RG + k

        def row_tags(slot):
            return feed_g[:, bass.ds(slot, 1), :].rearrange("p g (u r) -> p (g u) r", r=ROW)

        block = ctx.enter_context(nc.Block())

        @block.sync
        def _(sp):
            def load(g, slot, k):
                sp.dma_start(row_tags(slot)[:, :, 0:FEAT], edge_cols[:, bass.ds(g * GT, GT), :])\
                  .then_inc(load_sem[k], 16)

            def load_places(g, k):
                rows = places[bass.ds(g * GT, GT), :].rearrange("(a t) p -> a (t p)", a=1)
                sp.dma_start(place_rows[:, k, :], rows.to_broadcast([P, GT * P])).then_inc(place_sem[k], 16)

            sp.dma_start(src_row[:, 0:COLS], src[0:COLS * P].rearrange("(p t) -> p t", t=COLS)).then_inc(src_loaded, 16)
            sp.wait_ge(pool_set, 1)
            sp.dma_start(src_row[0:TAIL, COLS:COLS + 1],
                         src[COLS * P:EDGES].rearrange("(p t) -> p t", t=1)).then_inc(src_loaded, 16)
            for dst, part in x_windows(acc_w):
                if dst.shape[0] < P:
                    sp.wait_ge(pool_set, 3)
                sp.dma_start(dst, part).then_inc(x_loaded, 16)
            for k in range(RG):
                load(k, k, k)
            sp.wait_ge(placeT_copied, BLOCKS)
            for b in range(BLOCKS):
                n = min(P, TILES - b * P)
                sp.dma_start(places[b * P:b * P + n, :], placeT[0:n, b * P:(b + 1) * P]).then_inc(place_stored, 16)
            sp.wait_ge(place_stored, 16 * BLOCKS)
            for k in range(AHEAD):
                load_places(k, k)

            def pass_on(r, k, first, last=False):
                g = r * RG + k
                sp.wait_ge(load_sem[k], 16 * (r + 1))
                sp.wait_ge(place_sem[k], 16 * (r + 1))
                sp.sem_inc(landed, 1)
                if last and k + AHEAD >= RG:
                    return
                if not first or k + AHEAD >= RG:
                    sp.wait_ge(leaky_done, g + AHEAD - RG + 1)
                load_places(g + AHEAD, (k + AHEAD) % RG)

            for k in range(RG):
                pass_on(0, k, True)
                load(RG + k, RG + k, k)
            with sp.Fori(1, ROUNDS - 2) as r:
                for k in range(RG):
                    pass_on(r, k, False)
                    sp.wait_ge(scattered[k], 16 * GT * r)
                    load((r + 1) * RG + k, ((r + 1) % 2) * RG + k, k)
            r = ROUNDS - 2
            for k in range(RG):
                pass_on(r, k, False)
                sp.wait_ge(scattered[k], 16 * GT * r)
                slot = ((r + 1) % 2) * RG + k
                if k < RG - 1:
                    load((r + 1) * RG + k, slot, k)
                else:
                    last = feed_g[:, slot, :].rearrange("p (u r) -> p u r", r=ROW)
                    sp.dma_start(last[:, 0:LAST_FULL, 0:FEAT],
                                 edge_cols[:, COLS - LAST_FULL:COLS, :]).then_inc(load_sem[k], 16)
                    sp.wait_ge(load_sem[k], 16 * (r + 2))
                    sp.dma_start(last[0:TAIL, LAST_FULL, 0:FEAT], edge_attr[COLS * P:EDGES, :]).then_inc(load_sem[k], 16)
                    sp.wait_ge(load_sem[k], 16 * (r + 3))
            for k in range(RG):
                pass_on(ROUNDS - 1, k, False, last=True)

            for k in range(RG):
                sp.wait_ge(scattered[k], 16 * GT * ROUNDS)
            sp.wait_ge(self_saved, 16)
            sp.dma_start(feed[:, 0:WINDOWS * ROW], self_part).then_inc(final_loaded, 16)
            for dst, part in x_windows(fin_x):
                sp.dma_start(dst, part).then_inc(final_loaded, 16)

            out_w = out[0:(WINDOWS - 1) * P, :].rearrange("(w p) f -> p w f", p=P)
            for i in range(WINDOWS // RG):
                sp.wait_ge(result_done, RG * (i + 1))
                n = RG if i < WINDOWS // RG - 1 else RG - 1
                sp.dma_start(out_w[:, RG * i:RG * i + n, :], fin_x[:, RG * i:RG * i + n, 0:FEAT]).then_inc(stored, 16)
            sp.dma_start(out[(WINDOWS - 1) * P:NODES, :], fin_x[0:LAST_ROWS, WINDOWS - 1, 0:FEAT]).then_inc(stored, 16)
            sp.wait_ge(stored, 16 * (WINDOWS // RG + 1))

        @block.gpsimd
        def _(pool):
            pool.memset(src_row[:, COLS:TILES], WINDOWS * P).then_inc(pool_set, 1)
            pool.memset(acc_w[:, :, FEAT:ROW], 0.0).then_inc(pool_set, 1)
            pool.memset(acc_w[:, WINDOWS - 1, 0:FEAT], 0.0).then_inc(pool_set, 1)
            pool.iota(bucket_no[:, :], [[1, BUCKETS]], base=0, channel_multiplier=0,
                      allow_small_or_imprecise_dtypes=True).then_inc(pool_set, 1)
            pool.iota(lane[:, :], [[1, 1]], base=0, channel_multiplier=1,
                      allow_small_or_imprecise_dtypes=True).then_inc(pool_set, 1)
            pool.memset(below[:, :], 1.0).then_inc(pool_set, 1)
            pool.memset(above[:, :], 1.0).then_inc(pool_set, 1)
            pool.memset(ident[:, :], 0.0).then_inc(pool_set, 1)
            pool.memset(ident_bf[:, :], 0.0).then_inc(pool_set, 1)
            pool.memset(ones_bf[:, :], 1.0).then_inc(pool_set, 1)
            pool.memset(ones_row, 1.0).then_inc(pool_set, 1)
            pool.memset(ends[:, :], 0.0).then_inc(pool_set, 1)
            pool.memset(eps_col[:, :], EPS).then_inc(pool_set, 1)
            pool.memset(score_parts[:, :, :], 0.0).then_inc(pool_set, 1)
            pool.memset(zeros[:, :], 0.0).then_inc(pool_set, 1)
            pool.wait_ge(pool_set, 15)
            pool.affine_select(out=below[:, :], in_=below[:, :], compare_op=ALU.is_gt, fill=0.0, base=0,
                               pattern=[[1, P]], channel_multiplier=-1).then_inc(pool_set, 1)
            pool.affine_select(out=above[:, :], in_=above[:, :], compare_op=ALU.is_gt, fill=0.0, base=0,
                               pattern=[[-1, P]], channel_multiplier=1).then_inc(pool_set, 1)
            for m in (ident, ident_bf):
                pool.affine_select(out=m[:, :], in_=m[:, :], compare_op=ALU.not_equal, fill=1.0, base=0,
                                   pattern=[[-1, P]], channel_multiplier=1).then_inc(pool_set, 1)
            pool.iota(pair_no[:, :], [[1, MAXT + RT]], base=0, channel_multiplier=0,
                      allow_small_or_imprecise_dtypes=True).then_inc(pool_set, 1)
            pool.iota(psum_set[:, 0:(MAXT + RT) // (2 * GT) * 2 * GT], [[0, (MAXT + RT) // (2 * GT)], [3 * 512, 2], [0, GT]],
                      base=0, channel_multiplier=0, allow_small_or_imprecise_dtypes=True).then_inc(pool_set, 1)
            pool.iota(psum_set[:, (MAXT + RT) // (2 * GT) * 2 * GT:], [[3 * 512, (GT + (MAXT + RT) % (2 * GT)) // GT], [0, GT]],
                      base=0, channel_multiplier=0, allow_small_or_imprecise_dtypes=True).then_inc(pool_set, 1)
            tags = feed[:, :].rearrange("p (n r) -> p n r", r=ROW)
            pool.memset(tags[:, :, FEAT:ROW], 0.0).then_inc(pool_set, 1)
            pool.iota(node_id[:, :], [[P, BUCKETS], [1, ROW]], base=0, channel_multiplier=0,
                      allow_small_or_imprecise_dtypes=True).then_inc(pool_set, 1)

            def scatter_round(r, parity):
                for k in range(RG):
                    slot = parity * RG + k
                    pool.wait_ge(fed, r * RG + k + 1)
                    if not isinstance(r, int) or r > 0:
                        pool.wait_ge(scattered[k], r * (16 * GT))
                    pool.sem_inc(released, 1)
                    for u in range(GT):
                        n = slot * GT + u
                        pool.indirect_dma_start(
                            out=ordered, out_offset=bass.IndirectOffsetOnAxis(ap=dest[:, n:n + 1], axis=0),
                            in_=feed[:, n * ROW:(n + 1) * ROW], in_offset=None,
                        ).then_inc(scattered[k], 16)

            scatter_round(0, 0)
            scatter_round(1, 1)
            with pool.Fori(1, ROUNDS // 2) as i:
                scatter_round(2 * i, 0)
                scatter_round(2 * i + 1, 1)

        @block.scalar
        def _(act):
            act.dma_start(a_sb, a).then_inc(a_loaded, 16)
            act.dma_start(a2_row, a_2).then_inc(a_loaded, 16)
            for b in range(BLOCKS):
                n = min(P, TILES - b * P)
                act.wait_ge(placeT_done, b + 1)
                act.copy(placeT[0:n, b * P:(b + 1) * P], bank(b, 0, P, n)).then_inc(placeT_copied, 1)
            act.wait_ge(weights_step, 1)
            act.copy(A1w[:, 0:FEAT], bank(SCORES, 128, P)).then_inc(weights_copied, 1)
            act.copy(A2T[:, :], bank(SCORES, 256, P)).then_inc(weights_copied, 1)
            act.copy(a2_wide, bank(SCORES, 384, P)).then_inc(weights_copied, 1)
            act.wait_ge(weights_step, 2)
            act.copy(A1w[:, FEAT:FEAT + 1], bank(SCORES, 0, 1)).then_inc(weights_copied, 1)
            act.copy(edge_w[:, :], bank(SCORES, P, P)).then_inc(weights_copied, 1)

            def nodes():
                act.wait_ge(var_done, 1)
                act.activation(rstd[:, :], moments[:, :, 1], ACT.Sqrt, bias=eps_col[:, :]).then_inc(std_done, 1)
                act.wait_ge(rstd_done, 1)
                with act.Fori(0, WINDOWS // RG) as i:
                    for k in range(RG):
                        act.wait_ge(centredT_done, RG * i + k + 1)
                        act.copy(stageT[:, k, :], bank(k, 0, P)).then_inc(centredT_copied, 1)
                    for k in range(RG):
                        w = RG * i + k
                        act.wait_ge(self_done, w + 1)
                        act.activation(acc[:, bass.ds(w * ROW, FEAT + 1)], bank(k, P, FEAT + 1), ACT.Copy,
                                       scale=rstd[:, bass.ds(w, 1)]).then_inc(self_copied, 1)
                act.wait_ge(self_copied, WINDOWS)
                act.dma_start(self_part, acc[:, 0:WINDOWS * ROW]).then_inc(self_saved, 16)

            def scale_rows(g):
                tags = row_tags(g % SLOTS)
                act.wait_ge(leaky_done, g + 1)
                act.activation(tags[:, :, PROB], leaky[:, bass.ds(g % 2, 1), :].rearrange("p a t -> p (a t)"),
                               ACT.Exp, scale=-1.0).then_inc(prob_done, 1)
                act.activation(tags[:, :, SRC], src16[:, bass.ds(g * GT, GT)], ACT.Copy).then_inc(tagged, 1)
                act.wait_ge(prob_done, g + 1)
                for u in range(GT):
                    emb = tags[:, u, 0:FEAT]
                    last = act.activation(emb, emb, ACT.Copy, scale=tags[:, u, PROB:PROB + 1])
                last.then_inc(fed, 1)

            def feed_group(g):
                if not isinstance(g, int) or g > 0:
                    scale_rows(g - 1)
                if isinstance(g, int) and g == GROUPS - 1:
                    scale_rows(g)

            def read_back(c, r, k):
                g = (FIRST[c] + r) * RG + k
                act.dma_start(back_g[:, bass.ds(((FIRST[c] + r) % 2) * RG + k, 1), :],
                              ordered_g[bass.ds(g, 1), :, :].rearrange("g p r -> p g r")).then_inc(back_sem[k], 16)

            def start_chunk(c):
                if c == 0:
                    act.wait_ge(table_done, len(CHUNKS))
                    act.wait_ge(pool_set, 24)
                else:
                    act.wait_ge(step_done, STEP_ROUND[c] * RG)
                for q in range(RG):
                    act.wait_ge(scattered[q], 16 * GT * (FIRST[c] + CHUNKS[c]))
                for q in range(FETCH):
                    read_back(c, 0, q)

            def step(c, r, k):
                S, n = step_no(c, r, k), CHUNKS[c]
                slots = load_pairs(ENGINE.Activation, S, SLOT, 0, ACT_PAIRS)
                wins = load_pairs(ENGINE.Activation, S, WIN, 0, ACT_PAIRS)
                later = not isinstance(S, int) or S >= 2
                if later:
                    act.wait_ge(step_done, S - 1)
                ahead = (r, k + FETCH) if k + FETCH < RG else (r + 1, k + FETCH - RG)
                if not isinstance(r, int) or ahead[0] < n:
                    read_back(c, *ahead)
                if not isinstance(r, int) or r < n:
                    act.wait_ge(back_sem[k], 16 * (FIRST[c] + r + 1))
                if not isinstance(S, int) or S > 0:
                    act.wait_ge(act_hot, ACT_PAIRS * S)
                for u in range(ACT_PAIRS):
                    act.activation(dist[:, u, :], node_id[:, bass.ds(wins[u], P)], ACT.Abs, scale=-1.0,
                                   bias=back[:, bass.ds(slots[u] + SRC, 1)]).then_inc(dist_done, 1)
                act.wait_ge(dist_done, ACT_PAIRS * (S + 1))
                for u in range(ACT_PAIRS):
                    act.activation(hots[:, hot_buffer(k) * GT + u, :], dist[:, u, :], ACT.Relu, bias=1.0,
                                   scale=-1.0).then_inc(act_hot, 1)

            for what, *at in PLAN:
                if what == "nodes":
                    nodes()
                elif what == "feed":
                    run_feeds(act, *at, feed_group)
                elif what == "pairs":
                    if at[1] == 0:
                        start_chunk(at[0])
                    run_pairs(act, *at, step, feed_group)

            with act.Fori(0, WINDOWS // RG) as i:
                for k in range(RG):
                    act.wait_ge(scaledT_done, RG * i + k + 1)
                    act.copy(stageT[:, k, :], bank(k, 0, P)).then_inc(scaledT_copied, 1)

        @block.tensor
        def _(pe):
            pe.wait_ge(pool_set, 19)
            pe.wait_ge(place_made, 1)
            for b in range(BLOCKS):
                n = min(P, TILES - b * P)
                pe.matmul(bank(b, 0, P, n), place_bf[:, b * P:b * P + n], ident_bf[:, :], start=True, stop=True)\
                  .then_inc(placeT_done, 1)
            pe.wait_ge(a_loaded, 32)
            pe.wait_ge(placeT_copied, BLOCKS)
            pe.transpose(bank(SCORES, 128, P), a_sb[:, 0:FEAT], ident[:, :])
            pe.transpose(bank(SCORES, 256, P), a_sb[:, FEAT:2 * FEAT], ident[:, :])
            pe.matmul(bank(SCORES, 384, P), a2_row, ones_row, start=True, stop=True).then_inc(weights_step, 1)
            pe.wait_ge(weights_copied, 3)
            pe.matmul(bank(SCORES, 0, 1), a_sb[:, 0:FEAT], a2_wide[:, 0:1], start=True, stop=True)
            pe.matmul(bank(SCORES, P, P), a2_wide, a_sb[:, FEAT:2 * FEAT], start=True, stop=True)\
              .then_inc(weights_step, 1)

            def rank_sums(c):
                pe.wait_ge(ends_done, c + 1)
                pe.matmul(bank(RANKS, 0, BUCKETS), below[:, :], ends[:, 1:BUCKETS + 1], start=True, stop=False)
                pe.matmul(bank(RANKS, 0, BUCKETS), above[:, :], ends[:, 0:BUCKETS], start=False, stop=True)
                pe.matmul(bank(RANKS, 64, 1, BUCKETS), ends[:, 0:BUCKETS], ones_bf[:, 0:1], start=True, stop=True)\
                  .then_inc(shift_done, 1)

            def table_sums(c):
                npairs = CHUNKS[c] * RT + RT
                pe.wait_ge(started_done, c + 1)
                pe.matmul(bank(RANKS, P, npairs, 65), ones_bf[0:BUCKETS, 0:65], started[:, 0:npairs],
                          start=True, stop=True).then_inc(pairs_done, 1)

            def nodes():
                pe.wait_ge(weights_copied, 5)

                def products(i, first):
                    for k in range(RG):
                        pe.wait_ge(centred_done, RG * i + k + 1)
                        if not first:
                            pe.wait_ge(self_copied, RG * (i - 1) + k + 1)
                        pe.transpose(bank(k, 0, P), stage[:, k, :], ident[:, :]).then_inc(centredT_done, 1)
                    for k in range(RG):
                        pe.wait_ge(centredT_copied, RG * i + k + 1)
                        pe.matmul(bank(k, P, FEAT + 1), stageT[:, k, :], A1w[:, :], start=True, stop=True)\
                          .then_inc(self_done, 1)

                products(0, True)
                with pe.Fori(1, WINDOWS // RG) as i:
                    products(i, False)
                look_up(0)

            def look_up(g):
                pe.wait_ge(place_hot_done, g + 1)
                for u in range(GT):
                    for part in range(3):
                        last = pe.matmul(bank(SCORES, u * BUCKETS, BUCKETS), place_hot[:, u * P:(u + 1) * P],
                                         score_parts[:, part, :], start=part == 0, stop=part == 2)
                last.then_inc(node_scores, 1)

            def feed_group(g):
                if not isinstance(g, int) or g < GROUPS - 1:
                    look_up(g + 1)

            def step(c, r, k):
                S = step_no(c, r, k)
                slots = load_pairs(ENGINE.PE, S, SLOT, 0, GT)
                outs = load_pairs(ENGINE.PE, S, PLACE, 0, GT)
                if not isinstance(S, int) or S >= 2:
                    pe.wait_ge(acc_done, S - 1)
                for b in range(3):
                    pe.matmul(psum_sets[:, bass.ds(S % 2, 1), b, 0:PER_BANK * (FEAT + 1)], zeros[:, 0:P], zeros[:, :],
                              start=True, stop=False, skip_group_check=True)
                for u in range(GT):
                    if u == 0:
                        pe.wait_ge(act_hot, ACT_PAIRS * (S + 1))
                    if u == ACT_PAIRS:
                        pe.wait_ge(dve_hot, (GT - ACT_PAIRS) * (S + 1))
                    last = pe.matmul(psum[:, bass.ds(outs[u], FEAT + 1)], hots[:, hot_buffer(k) * GT + u, :],
                                     back[:, bass.ds(slots[u], FEAT + 1)], start=False, stop=u == GT - 1,
                                     skip_group_check=True)
                last.then_inc(step_done, 1)

            for what, *at in PLAN:
                if what == "count":
                    rank_sums(at[0])
                elif what == "rank":
                    table_sums(at[0])
                elif what == "nodes":
                    nodes()
                elif what == "feed":
                    run_feeds(pe, *at, feed_group)
                else:
                    run_pairs(pe, *at, step, feed_group)

            pe.wait_ge(acc_done, STEPS)
            with pe.Fori(0, WINDOWS // RG) as i:
                for k in range(RG):
                    pe.wait_ge(scaled_done, RG * i + k + 1)
                    pe.transpose(bank(k, 0, P), stage[:, k, :], ident[:, :]).then_inc(scaledT_done, 1)
                for k in range(RG):
                    pe.wait_ge(scaledT_copied, RG * i + k + 1)
                    pe.matmul(bank(k, P, P), stageT[:, k, :], A2T[:, :], start=True, stop=True).then_inc(out_ready, 1)

        @block.vector
        def _(dve):
            made = [0]

            def done(ins):
                made[0] += 1
                ins.then_inc(vec, 1)
                dve.wait_ge(vec, made[0])

            dve.wait_ge(src_loaded, 32)
            dve.wait_ge(pool_set, 20)
            dve.tensor_copy(src16[:, :], src_row[:, :]).then_inc(vec, 1)
            tmp = picked[:, 0:TILES].bitcast(I32)
            dve.tensor_scalar(tmp, src_row[:, :], 7, None, ALU.arith_shift_right).then_inc(vec, 1)
            dve.wait_ge(vec, 2)
            made[0] = 2
            done(dve.tensor_copy(bucket[:, :], tmp))
            done(dve.tensor_scalar(tmp, src_row[:, :], P - 1, None, ALU.bitwise_and))
            dve.tensor_copy(place_bf, tmp).then_inc(place_made, 1)
            dve.wait_ge(place_made, 1)

            def count_chunk(c):
                t0, tiles = FIRST[c] * RT, CHUNKS[c] * RT
                with dve.Fori(0, BUCKETS // BB) as i:
                    for k in range(BB):
                        dve.tensor_scalar(hot[:, bass.ds((i * BB + k) * tiles, tiles)], bucket[:, t0:t0 + tiles],
                                          bucket_no[:, bass.ds(i * BB + k, 1)], None, ALU.is_equal)\
                           .then_inc(hots_done, 1)
                dve.wait_ge(hots_done, BUCKETS * (c + 1))
                flat = BUCKETS * tiles
                done(dve.tensor_tensor_scan(count[:, 0:flat], hot[:, 0:flat], hot[:, 0:flat], 0.0, ALU.add, ALU.max))
                by_bucket = count[:, 0:flat].rearrange("p (b t) -> p b t", t=tiles)
                dve.tensor_copy(ends[:, 1:BUCKETS + 1], by_bucket[:, :, tiles - 1]).then_inc(ends_done, 1)

            def rank_chunk(c):
                t0, tiles = FIRST[c] * RT, CHUNKS[c] * RT
                dve.wait_ge(shift_done, c + 1)
                done(dve.tensor_scalar(shift[:, :], bank(RANKS, 0, BUCKETS), -1.0, None, ALU.add))
                n0 = made[0]
                with dve.Fori(0, BUCKETS // BB) as i:
                    for k in range(BB):
                        at = bass.ds((i * BB + k) * tiles, tiles)
                        dve.scalar_tensor_tensor(out=picked[:, k * tiles:(k + 1) * tiles], in0=count[:, at],
                                                 scalar=shift[:, bass.ds(i * BB + k, 1)], in1=hot[:, at],
                                                 op0=ALU.add, op1=ALU.mult).then_inc(vec, 1)
                    dve.wait_ge(vec, n0 + (BB + 1) * i + BB)
                    dve.tensor_reduce(partial[:, bass.ds(i * tiles, tiles)],
                                      picked[:, 0:BB * tiles].rearrange("p (b t) -> p t b", t=tiles),
                                      AX_X, ALU.add).then_inc(vec, 1)
                    dve.wait_ge(vec, n0 + (BB + 1) * (i + 1))
                made[0] = n0 + (BB + 1) * (BUCKETS // BB)
                rk = rank[:, 0:tiles]
                done(dve.tensor_reduce(rk, partial[:, 0:5 * tiles].rearrange("p (b t) -> p t b", t=tiles),
                                       AX_X, ALU.add))
                ri, pa, pb, pc = (v[:, 0:tiles] for v in (rank_i, part_a, part_b, part_c))
                done(dve.tensor_copy(ri, rk))
                low, mid = (P - 1).bit_length(), (GT - 1).bit_length()
                dve.tensor_scalar(pa, ri, low + mid, low + mid, ALU.arith_shift_right, ALU.logical_shift_left)\
                   .then_inc(vec, 1)
                dve.tensor_scalar(pb, ri, P - 1, mid, ALU.bitwise_and, ALU.logical_shift_left).then_inc(vec, 1)
                dve.tensor_scalar(pc, ri, low, GT - 1, ALU.arith_shift_right, ALU.bitwise_and).then_inc(vec, 1)
                made[0] += 3
                dve.wait_ge(vec, made[0])
                done(dve.tensor_tensor(pa, pa, pb, ALU.bitwise_or))
                done(dve.tensor_tensor(pa, pa, pc, ALU.bitwise_or))
                done(dve.tensor_scalar(src_row[:, t0:t0 + tiles], pa, float(FIRST[c] * RT * P), None, ALU.add))

                npairs = tiles + RT
                fp = first_pair
                done(dve.tensor_copy(first_pair_i[:, :], bank(RANKS, 64, 1, BUCKETS)))
                done(dve.tensor_scalar(first_pair_i[:, :], first_pair_i[:, :], low, None, ALU.arith_shift_right))
                done(dve.tensor_copy(fp[:, 0:1], first_pair_i[:, :]))
                done(dve.tensor_scalar(fp[:, 1:2], fp[:, 0:1], float(tiles - 1), lane[0:BUCKETS, :], ALU.min, ALU.add))
                dve.tensor_scalar(started[:, 0:npairs], pair_no[0:BUCKETS, 0:npairs], fp[:, 1:2], None, ALU.is_ge)\
                   .then_inc(started_done, 1)
                dve.wait_ge(pairs_done, c + 1)
                win, tile, wrap = (v[:, 0:npairs] for v in (row_win, row_tile, row_wrap))
                done(dve.tensor_scalar(win, bank(RANKS, P, npairs, 65), -1.0, None, ALU.add))
                done(dve.tensor_tensor(tile, pair_no[0:65, 0:npairs], win, ALU.subtract))
                done(dve.tensor_scalar(tile, tile, float(tiles - 1), float((FIRST[c] % 2) * RT), ALU.min, ALU.add))
                for _ in range((tiles + RT - 1) // (SLOTS * GT)):
                    done(dve.tensor_scalar(wrap, tile, float(SLOTS * GT), float(-SLOTS * GT), ALU.is_ge, ALU.mult))
                    done(dve.tensor_tensor(tile, tile, wrap, ALU.add))
                s0 = STEP_ROUND[c] * RG
                at = slice(s0 * GT, s0 * GT + npairs)
                dve.tensor_scalar(table[WIN:WIN + 1, at], win[WIN:WIN + 1], float(ROW), None, ALU.mult).then_inc(vec, 1)
                dve.tensor_scalar(table[SLOT:SLOT + 1, at], tile[SLOT:SLOT + 1], float(ROW), None, ALU.mult)\
                   .then_inc(vec, 1)
                made[0] += 2
                dve.wait_ge(vec, made[0])
                dve.wait_ge(pool_set, 22)
                steps = win.rearrange("q (s n) -> q s n", n=GT)
                since = tile.rearrange("q (s n) -> q s n", n=GT)
                done(dve.tensor_tensor(since, steps, steps[:, :, 0:1].to_broadcast([65, npairs // GT, GT]), ALU.subtract))
                wide = FEAT + 1
                done(dve.tensor_scalar(wrap, tile, float(PER_BANK), float(512 - PER_BANK * wide), ALU.is_ge, ALU.mult))
                done(dve.tensor_scalar(win, tile, float(2 * PER_BANK), float(512 - PER_BANK * wide), ALU.is_ge, ALU.mult))
                done(dve.tensor_tensor(wrap, wrap, win, ALU.add))
                done(dve.tensor_tensor(wrap, wrap, psum_set[:, (s0 % 2) * GT:(s0 % 2) * GT + npairs], ALU.add))
                done(dve.scalar_tensor_tensor(out=wrap, in0=tile, scalar=float(wide), in1=wrap, op0=ALU.mult, op1=ALU.add))
                dve.tensor_copy(table[PLACE:PLACE + 1, at], wrap[PLACE:PLACE + 1]).then_inc(table_done, 1)
                dve.wait_ge(table_done, c + 1)

            def nodes():
                dve.wait_ge(x_loaded, 32)
                dve.wait_ge(pool_set, 23)
                with dve.Fori(0, WINDOWS) as w:
                    dve.bn_stats(stats[:, bass.ds(w * 6, 6)], acc[:, bass.ds(w * ROW, FEAT)]).then_inc(stats_done, 1)
                dve.wait_ge(stats_done, WINDOWS)
                both = stats.rearrange("p (w s) -> p w s", s=6)
                mean, var, half_gap = moments[:, :, 0], moments[:, :, 1], kept[:, :]
                dve.tensor_tensor(mean, both[:, :, 1], both[:, :, 4], ALU.add).then_inc(vec, 1)
                dve.tensor_tensor(half_gap, both[:, :, 1], both[:, :, 4], ALU.subtract).then_inc(vec, 1)
                dve.tensor_tensor(var, both[:, :, 2], both[:, :, 5], ALU.add).then_inc(vec, 1)
                made[0] += 3
                dve.wait_ge(vec, made[0])
                done(dve.tensor_scalar(mean, mean, 0.5, None, ALU.mult))
                done(dve.tensor_scalar(half_gap, half_gap, 0.5, None, ALU.mult))
                done(dve.tensor_tensor(half_gap, half_gap, half_gap, ALU.mult))
                dve.scalar_tensor_tensor(out=var, in0=var, scalar=1.0 / FEAT, in1=half_gap, op0=ALU.mult,
                                         op1=ALU.add).then_inc(var_done, 1)
                dve.wait_ge(std_done, 1)
                dve.reciprocal(rstd[:, :], rstd[:, :]).then_inc(rstd_done, 1)
                dve.wait_ge(placeT_done, BLOCKS)

                def centre(i, k):
                    w = RG * i + k
                    dve.tensor_scalar(stage[:, k, :], acc[:, bass.ds(w * ROW, FEAT)],
                                      moments[:, bass.ds(w, 1), 0:1].rearrange("p w m -> p (w m)"), 0.0,
                                      ALU.subtract, ALU.max).then_inc(centred_done, 1)

                for k in range(RG):
                    centre(0, k)
                with dve.Fori(1, WINDOWS // RG) as i:
                    for k in range(RG):
                        dve.wait_ge(centredT_done, RG * (i - 1) + k + 1)
                        centre(i, k)
                dve.wait_ge(self_copied, WINDOWS)
                full, rest = acc_w[:, 0:WINDOWS, FEAT], score_rest[:, 0:WINDOWS]
                done(dve.tensor_copy(score_parts[:, 0, 0:WINDOWS], full))
                done(dve.tensor_tensor(rest, full, score_parts[:, 0, 0:WINDOWS], ALU.subtract))
                done(dve.tensor_copy(score_parts[:, 1, 0:WINDOWS], rest))
                done(dve.tensor_tensor(rest, rest, score_parts[:, 1, 0:WINDOWS], ALU.subtract))
                dve.tensor_copy(score_parts[:, 2, 0:WINDOWS], rest).then_inc(parts_done, 1)
                dve.wait_ge(parts_done, 1)
                dve.wait_ge(weights_copied, 5)
                start_group(0)

            def start_group(g):
                slot = g % SLOTS
                dve.wait_ge(landed, g + 1)
                dve.tensor_scalar(place_hot[:, :], place_rows[:, bass.ds(g % RG, 1), :].rearrange("p a n -> p (a n)"),
                                  lane[:, :], None, ALU.is_equal).then_inc(place_hot_done, 1)
                dve.tensor_copy(window[:, :], bucket[:, bass.ds(g * GT, GT)]).then_inc(window_copied, 1)
                for u in range(GT):
                    if u == 0 and (not isinstance(g, int) or g > 0):
                        dve.wait_ge(edge_dots, g * GT)
                    if u == JUNK:
                        dve.wait_ge(edge_dots, g * GT + JUNK)
                    dve.scalar_tensor_tensor(out=junk[:, u % JUNK, :],
                                             in0=feed[:, bass.ds((slot * GT + u) * ROW, FEAT)],
                                             scalar=1.0, in1=edge_w[:, :], op0=ALU.mult, op1=ALU.mult,
                                             accum_out=edge_score[:, u:u + 1]).then_inc(edge_dots, 1)

            def end_group(g):
                dve.tensor_copy(dest[:, bass.ds((g % SLOTS) * GT, GT)], src_row[:, bass.ds(g * GT, GT)])
                dve.wait_ge(node_scores, g + 1)
                dve.wait_ge(window_copied, g + 1)
                for u in range(GT):
                    dve.scalar_tensor_tensor(out=chosen[:, u, :], in0=bucket_no[:, :], scalar=window[:, u:u + 1],
                                             in1=bank(SCORES, u * BUCKETS, BUCKETS), op0=ALU.is_equal, op1=ALU.mult,
                                             accum_out=node_part[:, u:u + 1]).then_inc(selected, 1)
                dve.wait_ge(selected, (g + 1) * GT)
                dve.wait_ge(edge_dots, (g + 1) * GT)
                if not isinstance(g, int) or g > 0:
                    dve.wait_ge(leaky_done, g)
                dve.tensor_tensor(zed[:, :], node_part[:, :], edge_score[:, :], ALU.add).then_inc(zed_done, 1)
                dve.wait_ge(zed_done, g + 1)
                if not isinstance(g, int) or g > 1:
                    dve.wait_ge(prob_done, g - 1)
                dve.scalar_tensor_tensor(out=leaky[:, bass.ds(g % 2, 1), :].rearrange("p a t -> p (a t)"),
                                         in0=zed[:, :], scalar=SLOPE, in1=zed[:, :],
                                         op0=ALU.mult, op1=ALU.max).then_inc(leaky_done, 1)

            def feed_group(g):
                end_group(g)
                if not isinstance(g, int) or g < GROUPS - 1:
                    start_group(g + 1)

            def add_step(S):
                first_win, = load_pairs(ENGINE.DVE, S, WIN, 0, 1)
                dve.wait_ge(step_done, S + 1)
                if not isinstance(S, int) or S > 0:
                    dve.wait_ge(acc_done, S)
                sums = acc[:, bass.ds(first_win, SPAN * ROW)]\
                    .rearrange("p (b w r) -> p b w r", b=SPAN // PER_BANK, w=PER_BANK)[:, :, :, 0:FEAT + 1]
                new = psum_sets[:, bass.ds(S % 2, 1), :, 0:PER_BANK * (FEAT + 1)]\
                    .rearrange("p s b (w f) -> p (s b) w f", w=PER_BANK)
                dve.tensor_tensor(sums, sums, new, ALU.add).then_inc(acc_done, 1)

            def step(c, r, k):
                S = step_no(c, r, k)
                lag = not isinstance(S, int) or S >= 2
                if isinstance(S, int) and S == 0:
                    dve.wait_ge(self_saved, 16)
                    dve.memset(acc[:, :], 0.0).then_inc(acc_zero, 1)
                    dve.wait_ge(acc_zero, 1)
                    dve.wait_ge(pool_set, 24)
                wins = load_pairs(ENGINE.DVE, S, WIN, ACT_PAIRS, GT - ACT_PAIRS)
                slots = load_pairs(ENGINE.DVE, S, SLOT, ACT_PAIRS, GT - ACT_PAIRS)
                if not isinstance(r, int) or r < CHUNKS[c]:
                    dve.wait_ge(back_sem[k], 16 * (FIRST[c] + r + 1))
                if lag:
                    dve.wait_ge(step_done, S - 1)
                for u in range(ACT_PAIRS, GT):
                    dve.tensor_scalar(hots[:, hot_buffer(k) * GT + u, :], node_id[:, bass.ds(wins[u - ACT_PAIRS], P)],
                                      back[:, bass.ds(slots[u - ACT_PAIRS] + SRC, 1)], None, ALU.is_equal)\
                       .then_inc(dve_hot, 1)
                if lag:
                    add_step(S - 2)

            for what, *at in PLAN:
                if what == "count":
                    count_chunk(at[0])
                elif what == "rank":
                    rank_chunk(at[0])
                elif what == "nodes":
                    nodes()
                elif what == "feed":
                    run_feeds(dve, *at, feed_group)
                else:
                    run_pairs(dve, *at, step, feed_group)
            add_step(STEPS - 2)
            add_step(STEPS - 1)

            dve.wait_ge(acc_done, STEPS)
            total = acc_w[:, 0:WINDOWS, PROB]
            done(dve.tensor_scalar(denom[:, :], total, 0.0, TINY, ALU.is_equal, ALU.mult))
            done(dve.tensor_tensor(denom[:, :], denom[:, :], total, ALU.add))
            done(dve.reciprocal(inv[:, :], denom[:, :]))
            done(dve.tensor_tensor(kept[:, :], total, inv[:, :], ALU.mult))
            dve.wait_ge(final_loaded, 48)

            with dve.Fori(0, WINDOWS // RG) as i:
                for k in range(RG):
                    w = RG * i + k
                    dve.tensor_scalar(stage[:, k, :], acc[:, bass.ds(w * ROW, FEAT)], inv[:, bass.ds(w, 1)], None,
                                      ALU.mult).then_inc(scaled_done, 1)
                for k in range(RG):
                    w = RG * i + k
                    xw = feed[:, bass.ds((WINDOWS + w) * ROW, FEAT)]
                    dve.scalar_tensor_tensor(out=xw, in0=feed[:, bass.ds(w * ROW, FEAT)],
                                             scalar=kept[:, bass.ds(w, 1)], in1=xw, op0=ALU.mult,
                                             op1=ALU.add).then_inc(self_added, 1)
                for k in range(RG):
                    w = RG * i + k
                    xw = feed[:, bass.ds((WINDOWS + w) * ROW, FEAT)]
                    dve.wait_ge(out_ready, w + 1)
                    dve.wait_ge(self_added, w + 1)
                    dve.tensor_tensor(xw, xw, bank(k, P, P), ALU.add).then_inc(result_done, 1)


_INS = [("x", F32), ("src", I32), ("edge_attr_128", F32), ("L0_gnn_a", F32), ("L0_gnn_a_2", F32)]


def kernel(x, src, dst, edge_attr_128, L0_gnn_a, L0_gnn_a_2):
    import concourse.bacc as bacc
    from concourse.bass_utils import run_bass_kernel_spmd

    nc = bacc.Bacc("TRN2", target_bir_lowering=False, num_devices=1, dynamic_dma_scratch_size=8192)
    given = {"x": x, "src": src, "edge_attr_128": edge_attr_128, "L0_gnn_a": L0_gnn_a, "L0_gnn_a_2": L0_gnn_a_2}
    arrays, args = {}, []
    for name, dt in _INS:
        arr = np.ascontiguousarray(given[name])
        arrays[f"in_{name}"] = arr
        args.append(nc.dram_tensor(f"in_{name}", arr.shape, dt, kind="ExternalInput").ap())
    args.append(nc.dram_tensor("out_0", (NODES, FEAT), F32, kind="ExternalOutput").ap())
    gnn_kernel(nc, *args)
    r = run_bass_kernel_spmd(nc, [arrays], core_ids=[0])
    return r.results[0]["out_0"]
```

```python
from contextlib import ExitStack

import numpy as np

import concourse.bass as bass
from concourse import mybir

ALU = mybir.AluOpType
ACT = mybir.ActivationFunctionType
F32 = mybir.dt.float32
BF16 = mybir.dt.bfloat16
I16 = mybir.dt.int16
I32 = mybir.dt.int32
U32 = mybir.dt.uint32
ENGINE = mybir.EngineType

P = 128
NODES, EDGES, FEAT = 6250, 100000, 128
EPS = 1e-5
SLOPE = 0.2
TINY = 1e-12

WINDOWS = -(-NODES // P)
BUCKETS = WINDOWS + 1
LAST_ROWS = NODES - (WINDOWS - 1) * P

COLS = EDGES // P
TAIL = EDGES - COLS * P
GT = 8
RG = 7
RT = GT * RG
ROUNDS = -(-(COLS + 1) // RT)
TILES = ROUNDS * RT
GROUPS = ROUNDS * RG
LAST_FULL = COLS - (GROUPS - 1) * GT

CHUNKS = [2, 4, 4, 2, 2]
assert sum(CHUNKS) == ROUNDS and RT >= BUCKETS - 1
FIRST = [sum(CHUNKS[:c]) for c in range(len(CHUNKS))]
STEP_ROUND = [FIRST[c] + c for c in range(len(CHUNKS))]
STEP_ROUNDS = ROUNDS + len(CHUNKS)
STEPS = STEP_ROUNDS * RG
MAXT = max(CHUNKS) * RT

SLOTS = 2 * RG
ROW = FEAT + 4
PROB, SRC = FEAT, FEAT + 1
SPAN = 9
ACT_PAIRS = 4
BB = 10
ADD_LAG = 2
PER_BANK = 3
NO_CHECK = "the table's entries are clamped on chip"

FETCH = 5
AHEAD = 4
BLOCKS = -(-TILES // P)

PLAN = [
    ("stats",), ("count", 0), ("rank", 0), ("nodes",), ("feed", 0, 1), ("feed", 1, 1), ("feed", 2, 12),
    ("count", 1), ("rank", 1), ("feed", 14, 12), ("count", 2), ("feed", 26, 4), ("rank", 2),
    ("feed", 30, 5), ("count", 3), ("rank", 3), ("feed", 35, 7), ("count", 4), ("rank", 4), ("feed", 42, 5),
    ("pairs", 0, 0, 3, 47, 4), ("pairs", 1, 0, 5, 59, 4), ("pairs", 2, 0, 5, 79, 3),
    ("pairs", 3, 0, 1, 94, 3), ("pairs", 3, 1, 2, 97, 1), ("pairs", 3, 2, 3, 98, 0), ("pairs", 4, 0, 3, 98, 0),
]


def stretches(c, r0, r1):
    cuts = {r0, r1} | {r for r in (CHUNKS[c] - 1, CHUNKS[c]) if r0 < r < r1}
    if c == 0 and r0 == 0:
        cuts.add(1)
    cuts = sorted(cuts)
    return list(zip(cuts, cuts[1:]))


def run_feeds(engine, g0, n, feed_group):
    if n == 1:
        feed_group(g0)
    else:
        with engine.Fori(g0, g0 + n) as g:
            feed_group(g)


def run_pairs(engine, c, r0, r1, g0, per, step, feed_group):
    after = {(j + 1) * RG // per - 1: j for j in range(per)}
    for lo, hi in stretches(c, r0, r1):
        def body(r):
            for k in range(RG):
                step(c, r, k)
                if k in after:
                    feed_group(g0 - per * r0 + per * r + after[k])
        if hi - lo == 1:
            body(lo)
        else:
            with engine.Fori(lo, hi) as r:
                body(r)


def early(c):
    return 0 < c < len(CHUNKS) - 1


def hot_buffer(k):
    return 2 if k == RG - 1 else k % 2


def gnn_kernel(nc, x, src, edge_attr, a, a_2, out):
    ctx = ExitStack()
    with ctx:
        def sb(name, shape, dt):
            return ctx.enter_context(nc.sbuf_tensor(name, shape, dt))

        def sem(name):
            return ctx.enter_context(nc.semaphore(name))

        ordered = nc.dram_tensor("ordered_rows", [TILES * P, ROW], F32, kind="Internal").ap()
        self_part = nc.dram_tensor("self_part", [P, WINDOWS * ROW], F32, kind="Internal").ap()
        places = nc.dram_tensor("places", [TILES, P], BF16, kind="Internal").ap()

        feed = sb("feed", [P, SLOTS * GT * ROW], F32)
        back = sb("back", [P, SLOTS * GT * ROW], F32)
        acc = sb("acc", [P, (BUCKETS + SPAN - 1) * ROW], F32)
        node_id = sb("node_id", [P, BUCKETS * ROW], I16)
        table = sb("table", [65, (STEPS + ADD_LAG) * GT * 2], I32)
        hots = sb("hots", [P, 3 * GT, P], F32)
        dist = sb("dist", [P, ACT_PAIRS, P], BF16)
        place_rows = sb("place_rows", [P, RG, GT * P], BF16)
        place_hot = sb("place_hot", [P, GT * P], BF16)
        window = sb("window", [P, GT], F32)
        chosen = sb("chosen", [P, GT, BUCKETS], F32)
        score_parts = sb("score_parts", [P, 3, BUCKETS], BF16)
        score_rest = sb("score_rest", [P, BUCKETS], F32)
        src_row = sb("src_row", [P, TILES], I32)
        src16 = sb("src16", [P, TILES], I16)
        bucket = sb("bucket", [P, TILES], BF16)
        dest = sb("dest", [P, SLOTS * GT], U32)
        junk = sb("junk", [P, GT, P], F32)
        edge_w = sb("edge_w", [P, FEAT], F32)
        A2T = sb("A2T", [P, FEAT], F32)
        A1w = sb("A1w", [P, FEAT + 1], F32)
        ident = sb("ident", [P, P], F32)
        ident_bf = sb("ident_bf", [P, P], BF16)
        below = sb("below", [P, P], BF16)
        above = sb("above", [P, P], BF16)
        ones_bf = sb("ones_bf", [P, P], BF16)
        zeros = sb("zeros", [1, PER_BANK * (FEAT + 1)], BF16)
        lane = sb("lane", [P, 1], F32)
        bucket_no = sb("bucket_no", [P, BUCKETS], F32)
        bucket_no_bf = sb("bucket_no_bf", [P, BUCKETS], BF16)
        ends = sb("ends", [P, BUCKETS + 1], BF16)
        shift = sb("shift", [P, BUCKETS], F32)
        first_pair = sb("first_pair", [BUCKETS, 2], F32)
        first_pair_i = sb("first_pair_i", [BUCKETS, 1], I32)
        edge_score = sb("edge_score", [P, GT], F32)
        node_part = sb("node_part", [P, GT], F32)
        zed = sb("zed", [P, GT], F32)
        leaky = sb("leaky", [P, 2, GT], F32)
        moments = sb("moments", [P, WINDOWS, 2], F32)
        eps_col = sb("eps_col", [P, 1], F32)
        rstd = sb("rstd", [P, WINDOWS], F32)
        denom = sb("denom", [P, WINDOWS], F32)
        inv = sb("inv", [P, WINDOWS], F32)
        kept = sb("kept", [P, WINDOWS], F32)
        pair_no = sb("pair_no", [P, MAXT + RT], I16)
        psum_set = sb("psum_set", [65, MAXT + RT + GT], I16)

        half = back[:, :].bitcast(BF16)
        hot = half[:, 0:BUCKETS * MAXT]
        count = half[:, BUCKETS * MAXT:2 * BUCKETS * MAXT]
        f0 = BUCKETS * MAXT
        picked = back[:, f0:f0 + BB * MAXT]
        assert f0 + (BB + 1) * MAXT <= SLOTS * GT * ROW and BUCKETS % BB == 0 and RT < MAXT
        rank_i, part_a, part_b, part_c = (picked[:, n * MAXT:(n + 1) * MAXT].bitcast(I32) for n in range(4))
        row_win, row_tile, row_wrap = (picked[0:65, n * MAXT:(n + 2) * MAXT] for n in (4, 6, 8))
        started = back[0:BUCKETS, f0 + BB * MAXT:f0 + (BB + 1) * MAXT].bitcast(BF16)
        a_sb = hots[:, 14:16, :].rearrange("p c f -> p (c f)")
        a2_row = hots[0:1, 16, :]
        ones_row = hots[0:1, 17, :]
        a2_wide = hots[:, 18, :]
        place_bf = hots[:, 0:RG, :].bitcast(BF16).rearrange("p c f -> p (c f)")[:, 0:TILES]
        placeT = hots[:, 20:24, :].bitcast(BF16).rearrange("p c f -> p (c f)")[:, 0:BLOCKS * P]
        stats = feed[:, (SLOTS * GT - 3) * ROW:(SLOTS * GT - 3) * ROW + 6 * WINDOWS]

        psum = ctx.enter_context(nc.psum_tensor("psum", [P, 8 * 512], F32))
        psum_sets = psum[:, 0:6 * 512].rearrange("p (s b f) -> p s b f", s=2, b=3)
        SCORES, RANKS = 6, 7

        def bank(b, lo, n, rows=P):
            return psum[0:rows, b * 512 + lo:b * 512 + lo + n]

        names = """x_loaded a_loaded src_loaded pool_set released landed fed vec hots_done ends_done shift_done picks_done picks_added
            started_done pairs_done table_done place_made placeT_done placeT_copied place_stored
            weights_step weights_copied stats_done var_done std_done rstd_done centred_done
            centredT_done centredT_copied self_done self_copied self_saved parts_done acc_zero
            edge_dots place_hot_done window_copied selected zed_done node_scores leaky_done prob_done tagged act_hot dve_hot dist_done
            step_done acc_done inv_done scaled_done scaledT_done scaledT_copied out_ready self_added result_done
            final_loaded stored""".split()
        (x_loaded, a_loaded, src_loaded, pool_set, released, landed, fed, vec, hots_done, ends_done, shift_done, picks_done, picks_added,
         started_done, pairs_done, table_done, place_made, placeT_done, placeT_copied, place_stored,
         weights_step, weights_copied, stats_done, var_done, std_done, rstd_done, centred_done,
         centredT_done, centredT_copied, self_done, self_copied, self_saved, parts_done, acc_zero,
         edge_dots, place_hot_done, window_copied, selected, zed_done, node_scores, leaky_done, prob_done, tagged, act_hot, dve_hot, dist_done,
         step_done, acc_done, inv_done, scaled_done, scaledT_done, scaledT_copied, out_ready, self_added, result_done,
         final_loaded, stored) = (sem(n) for n in names)
        load_sem = [sem(f"load{k}") for k in range(RG)]
        place_sem = [sem(f"place{k}") for k in range(RG)]
        scattered = [sem(f"scattered{k}") for k in range(RG)]
        back_sem = [sem(f"back{k}") for k in range(RG)]

        feed_g = feed[:, :].rearrange("p (g r) -> p g r", r=GT * ROW)
        back_g = back[:, :].rearrange("p (g r) -> p g r", r=GT * ROW)
        edge_cols = edge_attr[0:COLS * P, :].rearrange("(p t) f -> p t f", t=COLS)
        ordered_g = ordered.rearrange("(g p u) r -> g p (u r)", p=P, u=GT)
        acc_w = acc[:, :].rearrange("p (w r) -> p w r", r=ROW)

        fin_x = feed[:, WINDOWS * ROW:2 * WINDOWS * ROW].rearrange("p (w r) -> p w r", r=ROW)
        stage = hots[:, 0:RG, :]
        stageT = hots[:, RG:2 * RG, :]

        def x_windows(dst):
            whole = x[0:(WINDOWS - 1) * P, :].rearrange("(w p) f -> p w f", p=P)
            return ((dst[:, 0:WINDOWS - 1, 0:FEAT], whole),
                    (dst[0:LAST_ROWS, WINDOWS - 1, 0:FEAT], x[(WINDOWS - 1) * P:NODES, :]))

        HOT, PRODUCT, ADD = 0, 32, 64
        LAST_WIN, LAST_SLOT = (BUCKETS - 1) * ROW, (SLOTS * GT - 1) * ROW
        MOST = {HOT: (LAST_WIN, LAST_SLOT), PRODUCT: (LAST_SLOT, 5 * 512 + (PER_BANK - 1) * (FEAT + 1)),
                ADD: (LAST_WIN, LAST_SLOT)}

        def load_pairs(engine, S, what, lo, n):
            got = []
            for at in range(2 * lo, 2 * (lo + n), 10):
                _, vals = nc.values_load_multi_w_load_instructions(
                    table[what:what + 1, bass.ds(S * (2 * GT) + at, min(10, 2 * (lo + n) - at))], engines=[engine],
                    min_val=0, max_val=max(MOST[what]), skip_runtime_bounds_check_because=NO_CHECK)
                got += vals
            first, second = (
                [nc.s_assert_within(v, 0, most, skip_runtime_bounds_check_because=NO_CHECK) for v in got[e::2]]
                for e, most in enumerate(MOST[what]))
            return first, second

        def step_no(c, r, k):
            return (STEP_ROUND[c] + r) * RG + k

        def row_tags(slot):
            return feed_g[:, bass.ds(slot, 1), :].rearrange("p g (u r) -> p (g u) r", r=ROW)

        block = ctx.enter_context(nc.Block())

        @block.sync
        def _(sp):
            def load(g, slot, k):
                sp.dma_start(row_tags(slot)[:, :, 0:FEAT], edge_cols[:, bass.ds(g * GT, GT), :])\
                  .then_inc(load_sem[k], 16)

            def load_places(g, k):
                rows = places[bass.ds(g * GT, GT), :].rearrange("(a t) p -> a (t p)", a=1)
                sp.dma_start(place_rows[:, k, :], rows.to_broadcast([P, GT * P])).then_inc(place_sem[k], 16)

            sp.dma_start(src_row[:, 0:COLS], src[0:COLS * P].rearrange("(p t) -> p t", t=COLS)).then_inc(src_loaded, 16)
            sp.wait_ge(pool_set, 1)
            sp.dma_start(src_row[0:TAIL, COLS:COLS + 1],
                         src[COLS * P:EDGES].rearrange("(p t) -> p t", t=1)).then_inc(src_loaded, 16)
            for dst, part in x_windows(acc_w):
                if dst.shape[0] < P:
                    sp.wait_ge(pool_set, 3)
                sp.dma_start(dst, part).then_inc(x_loaded, 16)
            for k in range(RG):
                load(k, k, k)
            sp.wait_ge(placeT_copied, BLOCKS)
            for b in range(BLOCKS):
                n = min(P, TILES - b * P)
                sp.dma_start(places[b * P:b * P + n, :], placeT[0:n, b * P:(b + 1) * P]).then_inc(place_stored, 16)
            sp.wait_ge(place_stored, 16 * BLOCKS)
            for k in range(AHEAD):
                load_places(k, k)

            def pass_on(r, k, first, last=False):
                g = r * RG + k
                sp.wait_ge(load_sem[k], 16 * (r + 1))
                sp.wait_ge(place_sem[k], 16 * (r + 1))
                sp.sem_inc(landed, 1)
                if last and k + AHEAD >= RG:
                    return
                if not first or k + AHEAD >= RG:
                    sp.wait_ge(leaky_done, g + AHEAD - RG + 1)
                load_places(g + AHEAD, (k + AHEAD) % RG)

            for k in range(RG):
                pass_on(0, k, True)
                load(RG + k, RG + k, k)
            with sp.Fori(1, ROUNDS - 2) as r:
                for k in range(RG):
                    pass_on(r, k, False)
                    sp.wait_ge(scattered[k], 16 * GT * r)
                    load((r + 1) * RG + k, ((r + 1) % 2) * RG + k, k)
            r = ROUNDS - 2
            for k in range(RG):
                pass_on(r, k, False)
                sp.wait_ge(scattered[k], 16 * GT * r)
                slot = ((r + 1) % 2) * RG + k
                if k < RG - 1:
                    load((r + 1) * RG + k, slot, k)
                else:
                    last = feed_g[:, slot, :].rearrange("p (u r) -> p u r", r=ROW)
                    sp.dma_start(last[:, 0:LAST_FULL, 0:FEAT],
                                 edge_cols[:, COLS - LAST_FULL:COLS, :]).then_inc(load_sem[k], 16)
                    sp.wait_ge(load_sem[k], 16 * (r + 2))
                    sp.dma_start(last[0:TAIL, LAST_FULL, 0:FEAT], edge_attr[COLS * P:EDGES, :]).then_inc(load_sem[k], 16)
                    sp.wait_ge(load_sem[k], 16 * (r + 3))
            for k in range(RG):
                pass_on(ROUNDS - 1, k, False, last=True)

            for k in range(RG):
                sp.wait_ge(scattered[k], 16 * GT * ROUNDS)
            sp.wait_ge(self_saved, 16)
            sp.wait_ge(back_sem[RG - 1], 16 * ROUNDS)
            sp.dma_start(feed[:, 0:WINDOWS * ROW], self_part).then_inc(final_loaded, 16)
            for dst, part in x_windows(fin_x):
                sp.dma_start(dst, part).then_inc(final_loaded, 16)

            out_w = out[0:(WINDOWS - 1) * P, :].rearrange("(w p) f -> p w f", p=P)
            for i in range(WINDOWS // RG):
                sp.wait_ge(result_done, RG * (i + 1))
                n = RG if i < WINDOWS // RG - 1 else RG - 1
                sp.dma_start(out_w[:, RG * i:RG * i + n, :], fin_x[:, RG * i:RG * i + n, 0:FEAT]).then_inc(stored, 16)
            sp.dma_start(out[(WINDOWS - 1) * P:NODES, :], fin_x[0:LAST_ROWS, WINDOWS - 1, 0:FEAT]).then_inc(stored, 16)
            sp.wait_ge(stored, 16 * (WINDOWS // RG + 1))

        @block.gpsimd
        def _(pool):
            pool.memset(src_row[:, COLS:TILES], WINDOWS * P).then_inc(pool_set, 1)
            pool.memset(acc_w[:, :, FEAT:ROW], 0.0).then_inc(pool_set, 1)
            pool.memset(acc_w[:, WINDOWS - 1, 0:FEAT], 0.0).then_inc(pool_set, 1)
            pool.iota(bucket_no[:, :], [[1, BUCKETS]], base=0, channel_multiplier=0,
                      allow_small_or_imprecise_dtypes=True).then_inc(pool_set, 1)
            pool.iota(bucket_no_bf[:, :], [[1, BUCKETS]], base=0, channel_multiplier=0,
                      allow_small_or_imprecise_dtypes=True).then_inc(pool_set, 1)
            pool.iota(lane[:, :], [[1, 1]], base=0, channel_multiplier=1,
                      allow_small_or_imprecise_dtypes=True).then_inc(pool_set, 1)
            pool.memset(below[:, :], 1.0).then_inc(pool_set, 1)
            pool.memset(above[:, :], 1.0).then_inc(pool_set, 1)
            pool.memset(ident[:, :], 0.0).then_inc(pool_set, 1)
            pool.memset(ident_bf[:, :], 0.0).then_inc(pool_set, 1)
            pool.memset(ones_bf[:, :], 1.0).then_inc(pool_set, 1)
            pool.memset(ones_row, 1.0).then_inc(pool_set, 1)
            pool.memset(ends[:, :], 0.0).then_inc(pool_set, 1)
            pool.memset(eps_col[:, :], EPS).then_inc(pool_set, 1)
            pool.memset(score_parts[:, :, :], 0.0).then_inc(pool_set, 1)
            pool.memset(zeros[:, :], 0.0).then_inc(pool_set, 1)
            pool.wait_ge(pool_set, 16)
            pool.affine_select(out=below[:, :], in_=below[:, :], compare_op=ALU.is_gt, fill=0.0, base=0,
                               pattern=[[1, P]], channel_multiplier=-1).then_inc(pool_set, 1)
            pool.affine_select(out=above[:, :], in_=above[:, :], compare_op=ALU.is_gt, fill=0.0, base=0,
                               pattern=[[-1, P]], channel_multiplier=1).then_inc(pool_set, 1)
            for m in (ident, ident_bf):
                pool.affine_select(out=m[:, :], in_=m[:, :], compare_op=ALU.not_equal, fill=1.0, base=0,
                                   pattern=[[-1, P]], channel_multiplier=1).then_inc(pool_set, 1)
            pool.iota(pair_no[:, :], [[1, MAXT + RT]], base=0, channel_multiplier=0,
                      allow_small_or_imprecise_dtypes=True).then_inc(pool_set, 1)
            pool.iota(psum_set[:, 0:(MAXT + RT) // (2 * GT) * 2 * GT], [[0, (MAXT + RT) // (2 * GT)], [3 * 512, 2], [0, GT]],
                      base=0, channel_multiplier=0, allow_small_or_imprecise_dtypes=True).then_inc(pool_set, 1)
            pool.iota(psum_set[:, (MAXT + RT) // (2 * GT) * 2 * GT:], [[3 * 512, (GT + (MAXT + RT) % (2 * GT)) // GT], [0, GT]],
                      base=0, channel_multiplier=0, allow_small_or_imprecise_dtypes=True).then_inc(pool_set, 1)
            tags = feed[:, :].rearrange("p (n r) -> p n r", r=ROW)
            pool.memset(tags[:, :, FEAT:ROW], 0.0).then_inc(pool_set, 1)
            pool.iota(node_id[:, :], [[P, BUCKETS], [1, ROW]], base=0, channel_multiplier=0,
                      allow_small_or_imprecise_dtypes=True).then_inc(pool_set, 1)

            def scatter_round(r, parity):
                for k in range(RG):
                    slot = parity * RG + k
                    pool.wait_ge(fed, r * RG + k + 1)
                    if not isinstance(r, int) or r > 0:
                        pool.wait_ge(scattered[k], r * (16 * GT))
                    pool.sem_inc(released, 1)
                    for u in range(GT):
                        n = slot * GT + u
                        pool.indirect_dma_start(
                            out=ordered, out_offset=bass.IndirectOffsetOnAxis(ap=dest[:, n:n + 1], axis=0),
                            in_=feed[:, n * ROW:(n + 1) * ROW], in_offset=None,
                        ).then_inc(scattered[k], 16)

            scatter_round(0, 0)
            scatter_round(1, 1)
            with pool.Fori(1, ROUNDS // 2) as i:
                scatter_round(2 * i, 0)
                scatter_round(2 * i + 1, 1)

        @block.scalar
        def _(act):
            act.dma_start(a_sb, a).then_inc(a_loaded, 16)
            act.dma_start(a2_row, a_2).then_inc(a_loaded, 16)
            for b in range(BLOCKS):
                n = min(P, TILES - b * P)
                act.wait_ge(placeT_done, b + 1)
                act.copy(placeT[0:n, b * P:(b + 1) * P], bank(b, 0, P, n)).then_inc(placeT_copied, 1)
            act.wait_ge(weights_step, 1)
            act.copy(A1w[:, 0:FEAT], bank(SCORES, 128, P)).then_inc(weights_copied, 1)
            act.copy(A2T[:, :], bank(SCORES, 256, P)).then_inc(weights_copied, 1)
            act.copy(a2_wide, bank(SCORES, 384, P)).then_inc(weights_copied, 1)
            act.wait_ge(weights_step, 2)
            act.copy(A1w[:, FEAT:FEAT + 1], bank(SCORES, 0, 1)).then_inc(weights_copied, 1)
            act.copy(edge_w[:, :], bank(SCORES, P, P)).then_inc(weights_copied, 1)

            def nodes():
                act.wait_ge(var_done, 1)
                act.activation(rstd[:, :], moments[:, :, 1], ACT.Sqrt, bias=eps_col[:, :]).then_inc(std_done, 1)
                act.wait_ge(rstd_done, 1)
                with act.Fori(0, WINDOWS // RG) as i:
                    for k in range(RG):
                        w = RG * i + k
                        act.activation(stage[:, k, :], acc[:, bass.ds(w * ROW, FEAT)], ACT.Relu,
                                       bias=moments[:, bass.ds(w, 1), 0:1].rearrange("p w m -> p (w m)"))\
                           .then_inc(centred_done, 1)
                    for k in range(RG):
                        act.wait_ge(centredT_done, RG * i + k + 1)
                        act.copy(stageT[:, k, :], bank(k, 0, P)).then_inc(centredT_copied, 1)
                    for k in range(RG):
                        w = RG * i + k
                        act.wait_ge(self_done, w + 1)
                        act.activation(acc[:, bass.ds(w * ROW, FEAT + 1)], bank(k, P, FEAT + 1), ACT.Copy,
                                       scale=rstd[:, bass.ds(w, 1)]).then_inc(self_copied, 1)
                act.wait_ge(self_copied, WINDOWS)
                act.dma_start(self_part, acc[:, 0:WINDOWS * ROW]).then_inc(self_saved, 16)

            def scale_rows(g):
                tags = row_tags(g % SLOTS)
                act.wait_ge(leaky_done, g + 1)
                act.activation(tags[:, :, PROB], leaky[:, bass.ds(g % 2, 1), :].rearrange("p a t -> p (a t)"),
                               ACT.Exp, scale=-1.0).then_inc(prob_done, 1)
                act.activation(tags[:, :, SRC], src16[:, bass.ds(g * GT, GT)], ACT.Copy).then_inc(tagged, 1)
                act.activation(dest[:, bass.ds((g % SLOTS) * GT, GT)], src_row[:, bass.ds(g * GT, GT)], ACT.Copy)
                act.wait_ge(prob_done, g + 1)
                for u in range(GT):
                    emb = tags[:, u, 0:FEAT]
                    last = act.activation(emb, emb, ACT.Copy, scale=tags[:, u, PROB:PROB + 1])
                last.then_inc(fed, 1)

            def feed_group(g):
                if not isinstance(g, int) or g > 0:
                    scale_rows(g - 1)
                if isinstance(g, int) and g == GROUPS - 1:
                    scale_rows(g)

            def read_back(c, r, k):
                g = (FIRST[c] + r) * RG + k
                act.dma_start(back_g[:, bass.ds(((FIRST[c] + r) % 2) * RG + k, 1), :],
                              ordered_g[bass.ds(g, 1), :, :].rearrange("g p r -> p g r")).then_inc(back_sem[k], 16)

            def scattered_chunk(c):
                for q in range(RG):
                    act.wait_ge(scattered[q], 16 * GT * (FIRST[c] + CHUNKS[c]))

            def start_chunk(c):
                if early(c):
                    return
                if c == 0:
                    act.wait_ge(table_done, len(CHUNKS))
                    act.wait_ge(pool_set, 25)
                else:
                    act.wait_ge(step_done, STEP_ROUND[c] * RG)
                scattered_chunk(c)
                for q in range(FETCH):
                    read_back(c, 0, q)

            def step(c, r, k):
                S, n = step_no(c, r, k), CHUNKS[c]
                wins, slots = load_pairs(ENGINE.Activation, S, HOT, 0, ACT_PAIRS)
                later = not isinstance(S, int) or S >= 2
                if later:
                    act.wait_ge(step_done, S - 1)
                if isinstance(r, int) and r == n and c + 1 < len(CHUNKS) and early(c + 1) and 1 <= k <= FETCH:
                    if k == 1:
                        scattered_chunk(c + 1)
                    read_back(c + 1, 0, k - 1)
                ahead = (r, k + FETCH) if k + FETCH < RG else (r + 1, k + FETCH - RG)
                if not isinstance(r, int) or ahead[0] < n:
                    read_back(c, *ahead)
                if not isinstance(r, int) or r < n:
                    act.wait_ge(back_sem[k], 16 * (FIRST[c] + r + 1))
                if not isinstance(S, int) or S > 0:
                    act.wait_ge(act_hot, ACT_PAIRS * S)
                for u in range(ACT_PAIRS):
                    act.activation(dist[:, u, :], node_id[:, bass.ds(wins[u], P)], ACT.Abs, scale=-1.0,
                                   bias=back[:, bass.ds(slots[u] + SRC, 1)]).then_inc(dist_done, 1)
                act.wait_ge(dist_done, ACT_PAIRS * (S + 1))
                for u in range(ACT_PAIRS):
                    act.activation(hots[:, hot_buffer(k) * GT + u, :], dist[:, u, :], ACT.Relu, bias=1.0,
                                   scale=-1.0).then_inc(act_hot, 1)

            for what, *at in PLAN:
                if what == "stats":
                    nodes()
                elif what == "feed":
                    run_feeds(act, *at, feed_group)
                elif what == "pairs":
                    if at[1] == 0:
                        start_chunk(at[0])
                    run_pairs(act, *at, step, feed_group)

            act.wait_ge(inv_done, 1)
            with act.Fori(0, WINDOWS // RG) as i:
                for k in range(RG):
                    w = RG * i + k
                    act.activation(stage[:, k, :], acc[:, bass.ds(w * ROW, FEAT)], ACT.Copy,
                                   scale=inv[:, bass.ds(w, 1)]).then_inc(scaled_done, 1)
                for k in range(RG):
                    act.wait_ge(scaledT_done, RG * i + k + 1)
                    act.copy(stageT[:, k, :], bank(k, 0, P)).then_inc(scaledT_copied, 1)

        @block.tensor
        def _(pe):
            pe.wait_ge(pool_set, 20)
            pe.wait_ge(place_made, 1)
            for b in range(BLOCKS):
                n = min(P, TILES - b * P)
                pe.matmul(bank(b, 0, P, n), place_bf[:, b * P:b * P + n], ident_bf[:, :], start=True, stop=True)\
                  .then_inc(placeT_done, 1)
            pe.wait_ge(a_loaded, 32)
            pe.wait_ge(placeT_copied, BLOCKS)
            pe.transpose(bank(SCORES, 128, P), a_sb[:, 0:FEAT], ident[:, :])
            pe.transpose(bank(SCORES, 256, P), a_sb[:, FEAT:2 * FEAT], ident[:, :])
            pe.matmul(bank(SCORES, 384, P), a2_row, ones_row, start=True, stop=True).then_inc(weights_step, 1)
            pe.wait_ge(weights_copied, 3)
            pe.matmul(bank(SCORES, 0, 1), a_sb[:, 0:FEAT], a2_wide[:, 0:1], start=True, stop=True)
            pe.matmul(bank(SCORES, P, P), a2_wide, a_sb[:, FEAT:2 * FEAT], start=True, stop=True)\
              .then_inc(weights_step, 1)

            def rank_sums(c):
                pe.wait_ge(ends_done, c + 1)
                pe.matmul(bank(RANKS, 0, BUCKETS), below[:, :], ends[:, 1:BUCKETS + 1], start=True, stop=False)
                pe.matmul(bank(RANKS, 0, BUCKETS), above[:, :], ends[:, 0:BUCKETS], start=False, stop=True)
                pe.matmul(bank(RANKS, 64, 1, BUCKETS), ends[:, 0:BUCKETS], ones_bf[:, 0:1], start=True, stop=True)\
                  .then_inc(shift_done, 1)

            def pick_sums(c, i):
                tiles = CHUNKS[c] * RT
                first = isinstance(i, int) and i == 0
                for k in range(BB):
                    pe.wait_ge(picks_done, c * BUCKETS + i * BB + k + 1)
                    pe.matmul(bank(RANKS, P, tiles), ident[:, :], picked[:, k * tiles:(k + 1) * tiles],
                              start=first and k == 0, stop=k == BB - 1, skip_group_check=True)\
                      .then_inc(picks_added, 1)

            def table_sums(c):
                npairs = CHUNKS[c] * RT + RT
                pe.wait_ge(started_done, c + 1)
                pe.matmul(bank(RANKS, P, npairs, 65), ones_bf[0:BUCKETS, 0:65], started[:, 0:npairs],
                          start=True, stop=True).then_inc(pairs_done, 1)

            def products(i):
                for k in range(RG):
                    pe.wait_ge(centred_done, RG * i + k + 1)
                    pe.transpose(bank(k, 0, P), stage[:, k, :], ident[:, :]).then_inc(centredT_done, 1)
                for k in range(RG):
                    pe.wait_ge(centredT_copied, RG * i + k + 1)
                    pe.matmul(bank(k, P, FEAT + 1), stageT[:, k, :], A1w[:, :], start=True, stop=True)\
                      .then_inc(self_done, 1)

            def look_up(g):
                pe.wait_ge(place_hot_done, g + 1)
                for u in range(GT):
                    for part in range(3):
                        last = pe.matmul(bank(SCORES, u * BUCKETS, BUCKETS), place_hot[:, u * P:(u + 1) * P],
                                         score_parts[:, part, :], start=part == 0, stop=part == 2)
                last.then_inc(node_scores, 1)

            def feed_group(g):
                if not isinstance(g, int) or g < GROUPS - 1:
                    look_up(g + 1)

            def step(c, r, k):
                S = step_no(c, r, k)
                slots, outs = load_pairs(ENGINE.PE, S, PRODUCT, 0, GT)
                if not isinstance(S, int) or S >= 2:
                    pe.wait_ge(acc_done, S - 1)
                for b in range(3):
                    pe.matmul(psum_sets[:, bass.ds(S % 2, 1), b, 0:PER_BANK * (FEAT + 1)], zeros[:, 0:P], zeros[:, :],
                              start=True, stop=False, skip_group_check=True)
                for u in range(GT):
                    if u == 0:
                        pe.wait_ge(act_hot, ACT_PAIRS * (S + 1))
                    if u == ACT_PAIRS:
                        pe.wait_ge(dve_hot, (GT - ACT_PAIRS) * (S + 1))
                    last = pe.matmul(psum[:, bass.ds(outs[u], FEAT + 1)], hots[:, hot_buffer(k) * GT + u, :],
                                     back[:, bass.ds(slots[u], FEAT + 1)], start=False, stop=u == GT - 1,
                                     skip_group_check=True)
                last.then_inc(step_done, 1)

            for what, *at in PLAN:
                if what == "count":
                    rank_sums(at[0])
                elif what == "stats":
                    pe.wait_ge(weights_copied, 5)
                    with pe.Fori(0, 2) as i:
                        products(i)
                elif what == "rank" and at[0] == 0:
                    for i in range(BUCKETS // BB):
                        pick_sums(0, i)
                        if i % 2 == 0:
                            products(2 + i // 2)
                    table_sums(0)
                    with pe.Fori(3 + (BUCKETS // BB - 1) // 2, WINDOWS // RG) as i:
                        products(i)
                elif what == "rank":
                    pick_sums(at[0], 0)
                    with pe.Fori(1, BUCKETS // BB) as i:
                        pick_sums(at[0], i)
                    table_sums(at[0])
                elif what == "nodes":
                    pe.wait_ge(parts_done, 1)
                    look_up(0)
                elif what == "feed":
                    run_feeds(pe, *at, feed_group)
                elif what == "pairs":
                    run_pairs(pe, *at, step, feed_group)

            pe.wait_ge(acc_done, STEPS)

            def last_products(i):
                for k in range(RG):
                    pe.wait_ge(scaled_done, RG * i + k + 1)
                    if not isinstance(i, int) or i > 0:
                        pe.wait_ge(result_done, RG * (i - 1) + k + 1)
                    pe.transpose(bank(k, 0, P), stage[:, k, :], ident[:, :]).then_inc(scaledT_done, 1)
                for k in range(RG):
                    pe.wait_ge(scaledT_copied, RG * i + k + 1)
                    pe.matmul(bank(k, P, P), stageT[:, k, :], A2T[:, :], start=True, stop=True).then_inc(out_ready, 1)

            last_products(0)
            with pe.Fori(1, WINDOWS // RG) as i:
                last_products(i)

        @block.vector
        def _(dve):
            made = [0]

            def done(ins):
                made[0] += 1
                ins.then_inc(vec, 1)
                dve.wait_ge(vec, made[0])

            dve.wait_ge(src_loaded, 32)
            dve.wait_ge(pool_set, 21)
            dve.tensor_copy(src16[:, :], src_row[:, :]).then_inc(vec, 1)
            tmp = picked[:, 0:TILES].bitcast(I32)
            dve.tensor_scalar(tmp, src_row[:, :], 7, None, ALU.arith_shift_right).then_inc(vec, 1)
            dve.wait_ge(vec, 2)
            made[0] = 2
            done(dve.tensor_copy(bucket[:, :], tmp))
            done(dve.tensor_scalar(tmp, src_row[:, :], P - 1, None, ALU.bitwise_and))
            dve.tensor_copy(place_bf, tmp).then_inc(place_made, 1)
            dve.wait_ge(place_made, 1)

            def count_chunk(c):
                t0, tiles = FIRST[c] * RT, CHUNKS[c] * RT
                flat = BUCKETS * tiles
                shape = [P, BUCKETS, tiles]
                dve.tensor_tensor(hot[:, 0:flat].rearrange("p (b t) -> p b t", t=tiles),
                                  bucket[:, t0:t0 + tiles].rearrange("p (a t) -> p a t", a=1).to_broadcast(shape),
                                  bucket_no_bf[:, :].rearrange("p (b a) -> p b a", a=1).to_broadcast(shape),
                                  ALU.is_equal).then_inc(hots_done, 1)
                dve.wait_ge(hots_done, c + 1)
                done(dve.tensor_tensor_scan(count[:, 0:flat], hot[:, 0:flat], hot[:, 0:flat], 0.0, ALU.add, ALU.max))
                by_bucket = count[:, 0:flat].rearrange("p (b t) -> p b t", t=tiles)
                dve.tensor_copy(ends[:, 1:BUCKETS + 1], by_bucket[:, :, tiles - 1]).then_inc(ends_done, 1)

            def rank_chunk(c):
                t0, tiles = FIRST[c] * RT, CHUNKS[c] * RT
                dve.wait_ge(shift_done, c + 1)
                done(dve.tensor_scalar(shift[:, :], bank(RANKS, 0, BUCKETS), -1.0, None, ALU.add))

                for b in range(BUCKETS):
                    n, k, at = c * BUCKETS + b, b % BB, slice(b * tiles, (b + 1) * tiles)
                    if n >= BB:
                        dve.wait_ge(picks_added, n - BB + 1)
                    dve.scalar_tensor_tensor(out=picked[:, k * tiles:(k + 1) * tiles], in0=count[:, at],
                                             scalar=shift[:, b:b + 1], in1=hot[:, at],
                                             op0=ALU.add, op1=ALU.mult).then_inc(picks_done, 1)
                dve.wait_ge(picks_added, (c + 1) * BUCKETS)
                ri, pa, pb, pc = (v[:, 0:tiles] for v in (rank_i, part_a, part_b, part_c))
                done(dve.tensor_copy(ri, bank(RANKS, P, tiles)))
                low, mid = (P - 1).bit_length(), (GT - 1).bit_length()
                dve.tensor_scalar(pa, ri, low + mid, low + mid, ALU.arith_shift_right, ALU.logical_shift_left)\
                   .then_inc(vec, 1)
                dve.tensor_scalar(pb, ri, P - 1, mid, ALU.bitwise_and, ALU.logical_shift_left).then_inc(vec, 1)
                dve.tensor_scalar(pc, ri, low, GT - 1, ALU.arith_shift_right, ALU.bitwise_and).then_inc(vec, 1)
                made[0] += 3
                dve.wait_ge(vec, made[0])
                done(dve.tensor_tensor(pa, pa, pb, ALU.bitwise_or))
                done(dve.tensor_tensor(pa, pa, pc, ALU.bitwise_or))
                done(dve.tensor_scalar(src_row[:, t0:t0 + tiles], pa, float(FIRST[c] * RT * P), None, ALU.add))

                npairs = tiles + RT
                fp = first_pair
                done(dve.tensor_copy(first_pair_i[:, :], bank(RANKS, 64, 1, BUCKETS)))
                done(dve.tensor_scalar(first_pair_i[:, :], first_pair_i[:, :], low, None, ALU.arith_shift_right))
                done(dve.tensor_copy(fp[:, 0:1], first_pair_i[:, :]))
                done(dve.tensor_scalar(fp[:, 1:2], fp[:, 0:1], float(tiles - 1), lane[0:BUCKETS, :], ALU.min, ALU.add))
                dve.tensor_scalar(started[:, 0:npairs], pair_no[0:BUCKETS, 0:npairs], fp[:, 1:2], None, ALU.is_ge)\
                   .then_inc(started_done, 1)
                dve.wait_ge(pairs_done, c + 1)
                win, tile, wrap = (v[:, 0:npairs] for v in (row_win, row_tile, row_wrap))
                done(dve.tensor_scalar(win, bank(RANKS, P, npairs, 65), -1.0, None, ALU.add))
                done(dve.tensor_tensor(tile, pair_no[0:65, 0:npairs], win, ALU.subtract))
                done(dve.tensor_scalar(tile, tile, float(tiles - 1), float((FIRST[c] % 2) * RT), ALU.min, ALU.add))
                for _ in range((tiles + RT - 1) // (SLOTS * GT)):
                    done(dve.tensor_scalar(wrap, tile, float(SLOTS * GT), float(-SLOTS * GT), ALU.is_ge, ALU.mult))
                    done(dve.tensor_tensor(tile, tile, wrap, ALU.add))
                s0 = STEP_ROUND[c] * RG
                pairs = table[:, s0 * 2 * GT:(s0 * GT + npairs) * 2].rearrange("q (n e) -> q n e", e=2)
                steps = win.rearrange("q (s n) -> q s n", n=GT)
                since = tile.rearrange("q (s n) -> q s n", n=GT)
                s1 = s0 + npairs // GT
                adds = table[ADD:ADD + 1, (s0 + ADD_LAG) * 2 * GT:(s1 + ADD_LAG) * 2 * GT]\
                    .rearrange("q (s n) -> q s n", n=2 * GT)
                own = pairs[ADD:ADD + 1].rearrange("q (s n) e -> q s n e", n=GT)
                taken = slice(1, 1 + GT - ACT_PAIRS)
                row = float(ROW)
                dve.tensor_scalar(pairs[HOT:HOT + 1, :, 0], win[HOT:HOT + 1], row, None, ALU.mult).then_inc(vec, 1)
                dve.tensor_scalar(pairs[HOT:HOT + 1, :, 1], tile[HOT:HOT + 1], row, None, ALU.mult).then_inc(vec, 1)
                dve.tensor_scalar(pairs[PRODUCT:PRODUCT + 1, :, 0], tile[PRODUCT:PRODUCT + 1], row, None, ALU.mult)\
                   .then_inc(vec, 1)
                dve.tensor_scalar(adds[:, :, 0], steps[ADD:ADD + 1, :, 0], row, None, ALU.mult).then_inc(vec, 1)
                dve.tensor_scalar(own[:, :, taken, 0], steps[ADD:ADD + 1, :, ACT_PAIRS:], row, None, ALU.mult)\
                   .then_inc(vec, 1)
                dve.tensor_scalar(own[:, :, taken, 1], since[ADD:ADD + 1, :, ACT_PAIRS:], row, None, ALU.mult)\
                   .then_inc(vec, 1)
                made[0] += 6
                dve.wait_ge(vec, made[0])
                dve.wait_ge(pool_set, 23)
                done(dve.tensor_tensor(since, steps, steps[:, :, 0:1].to_broadcast([65, npairs // GT, GT]), ALU.subtract))
                done(dve.tensor_scalar(adds[:, :, 1], since[ADD:ADD + 1, :, GT - 1], row, None, ALU.mult))
                wide = FEAT + 1
                done(dve.tensor_scalar(wrap, tile, float(PER_BANK), float(512 - PER_BANK * wide), ALU.is_ge, ALU.mult))
                done(dve.tensor_scalar(win, tile, float(2 * PER_BANK), float(512 - PER_BANK * wide), ALU.is_ge, ALU.mult))
                done(dve.tensor_tensor(wrap, wrap, win, ALU.add))
                done(dve.tensor_tensor(wrap, wrap, psum_set[:, (s0 % 2) * GT:(s0 % 2) * GT + npairs], ALU.add))
                done(dve.scalar_tensor_tensor(out=wrap, in0=tile, scalar=float(wide), in1=wrap, op0=ALU.mult, op1=ALU.add))
                dve.tensor_copy(pairs[PRODUCT:PRODUCT + 1, :, 1], wrap[PRODUCT:PRODUCT + 1]).then_inc(table_done, 1)
                dve.wait_ge(table_done, c + 1)

            def node_stats():
                dve.wait_ge(x_loaded, 32)
                dve.wait_ge(pool_set, 24)
                for w in range(WINDOWS):
                    dve.bn_stats(stats[:, w * 6:(w + 1) * 6], acc[:, w * ROW:w * ROW + FEAT]).then_inc(stats_done, 1)
                dve.wait_ge(stats_done, WINDOWS)
                both = stats.rearrange("p (w s) -> p w s", s=6)
                mean, var, half_gap = moments[:, :, 0], moments[:, :, 1], kept[:, :]
                dve.tensor_tensor(mean, both[:, :, 1], both[:, :, 4], ALU.add).then_inc(vec, 1)
                dve.tensor_tensor(half_gap, both[:, :, 1], both[:, :, 4], ALU.subtract).then_inc(vec, 1)
                dve.tensor_tensor(var, both[:, :, 2], both[:, :, 5], ALU.add).then_inc(vec, 1)
                made[0] += 3
                dve.wait_ge(vec, made[0])
                done(dve.tensor_scalar(mean, mean, -0.5, None, ALU.mult))
                done(dve.tensor_scalar(half_gap, half_gap, 0.5, None, ALU.mult))
                done(dve.tensor_tensor(half_gap, half_gap, half_gap, ALU.mult))
                dve.scalar_tensor_tensor(out=var, in0=var, scalar=1.0 / FEAT, in1=half_gap, op0=ALU.mult,
                                         op1=ALU.add).then_inc(var_done, 1)
                dve.wait_ge(std_done, 1)
                dve.reciprocal(rstd[:, :], rstd[:, :]).then_inc(rstd_done, 1)

            def nodes():
                dve.wait_ge(weights_copied, 5)
                start_group(0)
                dve.wait_ge(self_copied, WINDOWS)
                full, rest = acc_w[:, 0:WINDOWS, FEAT], score_rest[:, 0:WINDOWS]
                done(dve.tensor_copy(score_parts[:, 0, 0:WINDOWS], full))
                done(dve.tensor_tensor(rest, full, score_parts[:, 0, 0:WINDOWS], ALU.subtract))
                done(dve.tensor_copy(score_parts[:, 1, 0:WINDOWS], rest))
                done(dve.tensor_tensor(rest, rest, score_parts[:, 1, 0:WINDOWS], ALU.subtract))
                dve.tensor_copy(score_parts[:, 2, 0:WINDOWS], rest).then_inc(parts_done, 1)

            def start_group(g):
                slot = g % SLOTS
                dve.wait_ge(landed, g + 1)
                dve.tensor_scalar(place_hot[:, :], place_rows[:, bass.ds(g % RG, 1), :].rearrange("p a n -> p (a n)"),
                                  lane[:, :], None, ALU.is_equal).then_inc(place_hot_done, 1)
                dve.tensor_copy(window[:, :], bucket[:, bass.ds(g * GT, GT)]).then_inc(window_copied, 1)
                for u in range(GT):
                    dve.scalar_tensor_tensor(out=junk[:, u, :],
                                             in0=feed[:, bass.ds((slot * GT + u) * ROW, FEAT)],
                                             scalar=1.0, in1=edge_w[:, :], op0=ALU.mult, op1=ALU.mult,
                                             accum_out=edge_score[:, u:u + 1]).then_inc(edge_dots, 1)

            def end_group(g):
                dve.wait_ge(node_scores, g + 1)
                dve.wait_ge(window_copied, g + 1)
                for u in range(GT):
                    dve.scalar_tensor_tensor(out=chosen[:, u, :], in0=bucket_no[:, :], scalar=window[:, u:u + 1],
                                             in1=bank(SCORES, u * BUCKETS, BUCKETS), op0=ALU.is_equal, op1=ALU.mult,
                                             accum_out=node_part[:, u:u + 1]).then_inc(selected, 1)
                dve.wait_ge(selected, (g + 1) * GT)
                dve.wait_ge(edge_dots, (g + 1) * GT)
                if not isinstance(g, int) or g > 0:
                    dve.wait_ge(leaky_done, g)
                dve.tensor_tensor(zed[:, :], node_part[:, :], edge_score[:, :], ALU.add).then_inc(zed_done, 1)
                dve.wait_ge(zed_done, g + 1)
                if not isinstance(g, int) or g > 1:
                    dve.wait_ge(prob_done, g - 1)
                dve.scalar_tensor_tensor(out=leaky[:, bass.ds(g % 2, 1), :].rearrange("p a t -> p (a t)"),
                                         in0=zed[:, :], scalar=SLOPE, in1=zed[:, :],
                                         op0=ALU.mult, op1=ALU.max).then_inc(leaky_done, 1)

            def feed_group(g):
                end_group(g)
                if not isinstance(g, int) or g < GROUPS - 1:
                    start_group(g + 1)

            def add_step(S, first_win, others):
                sums = acc[:, bass.ds(first_win, SPAN * ROW)]\
                    .rearrange("p (b w r) -> p b w r", b=SPAN // PER_BANK, w=PER_BANK)[:, :, :, 0:FEAT + 1]
                new = psum_sets[:, bass.ds(S % 2, 1), :, 0:PER_BANK * (FEAT + 1)]\
                    .rearrange("p s b (w f) -> p (s b) w f", w=PER_BANK)

                def wait():
                    dve.wait_ge(step_done, S + 1)
                    if not isinstance(S, int) or S > 0:
                        dve.wait_ge(acc_done, S)

                with dve.If(others >= PER_BANK * ROW):
                    wait()
                    dve.tensor_tensor(sums[:, 1:], sums[:, 1:], new[:, 1:], ALU.add)
                wait()
                dve.tensor_tensor(sums[:, 0], sums[:, 0], new[:, 0], ALU.add).then_inc(acc_done, 1)

            def step(c, r, k):
                S = step_no(c, r, k)
                lag = not isinstance(S, int) or S >= ADD_LAG
                if isinstance(S, int) and S == 0:
                    dve.wait_ge(self_saved, 16)
                    dve.memset(acc[:, :], 0.0).then_inc(acc_zero, 1)
                    dve.wait_ge(acc_zero, 1)
                    dve.wait_ge(pool_set, 25)
                skip = 0 if lag else 1
                wins, slots = load_pairs(ENGINE.DVE, S, ADD, skip, 1 + GT - ACT_PAIRS - skip)
                if lag:
                    add_step(S - ADD_LAG, wins.pop(0), slots.pop(0))
                if not isinstance(r, int) or r < CHUNKS[c]:
                    dve.wait_ge(back_sem[k], 16 * (FIRST[c] + r + 1))
                for u in range(ACT_PAIRS, GT):
                    dve.tensor_scalar(hots[:, hot_buffer(k) * GT + u, :], node_id[:, bass.ds(wins[u - ACT_PAIRS], P)],
                                      back[:, bass.ds(slots[u - ACT_PAIRS] + SRC, 1)], None, ALU.is_equal)\
                       .then_inc(dve_hot, 1)

            for what, *at in PLAN:
                if what == "count":
                    count_chunk(at[0])
                elif what == "rank":
                    rank_chunk(at[0])
                elif what == "stats":
                    node_stats()
                elif what == "nodes":
                    nodes()
                elif what == "feed":
                    run_feeds(dve, *at, feed_group)
                elif what == "pairs":
                    run_pairs(dve, *at, step, feed_group)
            for S in range(STEPS - ADD_LAG, STEPS):
                (first,), (others,) = load_pairs(ENGINE.DVE, S + ADD_LAG, ADD, 0, 1)
                add_step(S, first, others)

            dve.wait_ge(acc_done, STEPS)
            total = acc_w[:, 0:WINDOWS, PROB]
            done(dve.tensor_scalar(denom[:, :], total, 0.0, TINY, ALU.is_equal, ALU.mult))
            done(dve.tensor_tensor(denom[:, :], denom[:, :], total, ALU.add))
            dve.reciprocal(inv[:, :], denom[:, :]).then_inc(inv_done, 1)
            dve.wait_ge(inv_done, 1)
            done(dve.tensor_tensor(kept[:, :], total, inv[:, :], ALU.mult))
            dve.wait_ge(final_loaded, 48)

            with dve.Fori(0, WINDOWS // RG) as i:
                for k in range(RG):
                    w = RG * i + k
                    xw = feed[:, bass.ds((WINDOWS + w) * ROW, FEAT)]
                    dve.scalar_tensor_tensor(out=xw, in0=feed[:, bass.ds(w * ROW, FEAT)],
                                             scalar=kept[:, bass.ds(w, 1)], in1=xw, op0=ALU.mult,
                                             op1=ALU.add).then_inc(self_added, 1)
                for k in range(RG):
                    w = RG * i + k
                    xw = feed[:, bass.ds((WINDOWS + w) * ROW, FEAT)]
                    dve.wait_ge(out_ready, w + 1)
                    dve.wait_ge(self_added, w + 1)
                    dve.tensor_tensor(xw, xw, bank(k, P, P), ALU.add).then_inc(result_done, 1)


_INS = [("x", F32), ("src", I32), ("edge_attr_128", F32), ("L0_gnn_a", F32), ("L0_gnn_a_2", F32)]


def kernel(x, src, dst, edge_attr_128, L0_gnn_a, L0_gnn_a_2):
    import concourse.bacc as bacc
    from concourse.bass_utils import run_bass_kernel_spmd

    nc = bacc.Bacc("TRN2", target_bir_lowering=False, num_devices=1, dynamic_dma_scratch_size=8192)
    given = {"x": x, "src": src, "edge_attr_128": edge_attr_128, "L0_gnn_a": L0_gnn_a, "L0_gnn_a_2": L0_gnn_a_2}
    arrays, args = {}, []
    for name, dt in _INS:
        arr = np.ascontiguousarray(given[name])
        arrays[f"in_{name}"] = arr
        args.append(nc.dram_tensor(f"in_{name}", arr.shape, dt, kind="ExternalInput").ap())
    args.append(nc.dram_tensor("out_0", (NODES, FEAT), F32, kind="ExternalOutput").ap())
    gnn_kernel(nc, *args)
    r = run_bass_kernel_spmd(nc, [arrays], core_ids=[0])
    return r.results[0]["out_0"]
```
